# Optimizing a Trainium2 kernel written in Bass

```python
import numpy as np
import jax
import jax.numpy as jnp

def _softmax(x, axis=-1):
    return jax.nn.softmax(x, axis=axis)

def _gelu(x):
    return jax.nn.gelu(x, approximate=True)

def _silu(x):
    return jax.nn.silu(x)

def _sigmoid(x):
    return jax.nn.sigmoid(x)

def _layernorm(x, axis=-1, eps=1e-05):
    m = jnp.mean(x, axis=axis, keepdims=True)
    v = jnp.var(x, axis=axis, keepdims=True)
    return (x - m) / jnp.sqrt(v + eps)

def _scatter_add(tgt, idx, src, axis=0):
    return tgt.at[idx].add(src)

def _segment_sum(src, seg, n):
    return jax.ops.segment_sum(src, seg, n)
kernel_name = 'mk_recurrent_d1_jaxref_r4_7b014a'

def setup_inputs(seed: int=0):
    np.random.seed(seed)
    _w = jnp.asarray

    def _L0_attn_setup():
        import jax, jax.numpy as jnp
        import numpy as np
        import math
        D_MODEL = 512
        D_STATE = 16
        D_CONV = 4
        EXPAND = 2
        D_INNER = EXPAND * D_MODEL
        DT_RANK = math.ceil(D_MODEL / 16)
        BATCH = 2
        SEQLEN = 256
        DT_MIN, DT_MAX = (0.001, 0.1)

        def _hadamard_matrix(n):
            H = np.array([[1.0]], dtype=np.float32)
            while H.shape[0] < n:
                H = np.block([[H, H], [H, -H]])
            return H
        _H = jnp.asarray(_hadamard_matrix(D_INNER) / math.sqrt(D_INNER))

        def _selective_scan(u, delta, A, Bm, Cm, D, z):
            xs = (jnp.moveaxis(delta, 2, 0), jnp.moveaxis(u, 2, 0), jnp.moveaxis(Bm, 2, 0), jnp.moveaxis(Cm, 2, 0))
            b = u.shape[0]
            state0 = jnp.zeros((b, A.shape[0], A.shape[1]), dtype=u.dtype)

            def step(state, inp):
                dt_t, u_t, B_t, C_t = inp
                dA = jnp.exp(dt_t[:, :, None] * A[None])
                dBu = (dt_t * u_t)[:, :, None] * B_t[:, None, :]
                state = state * dA + dBu
                y_t = jnp.einsum('bdn,bn->bd', state, C_t)
                return (state, y_t)
            _, ys = jax.lax.scan(step, state0, xs)
            y = jnp.moveaxis(ys, 0, 2)
            y = y + D[None, :, None] * u
            return y * jax.nn.silu(z)
        key = jax.random.key(seed)
        ks = jax.random.split(key, 10)
        hidden_states = jax.random.normal(ks[0], (BATCH, SEQLEN, D_MODEL), dtype=jnp.float32)
        W_in = jax.random.normal(ks[1], (2 * D_INNER, D_MODEL), dtype=jnp.float32) * 0.02
        conv_w = jax.random.normal(ks[2], (D_INNER, D_CONV), dtype=jnp.float32) * 0.2
        conv_b = jax.random.normal(ks[3], (D_INNER,), dtype=jnp.float32) * 0.02
        W_x = jax.random.normal(ks[4], (DT_RANK + 2 * D_STATE, D_INNER), dtype=jnp.float32) * 0.02
        dt_init_std = DT_RANK ** (-0.5)
        W_dt = jax.random.uniform(ks[5], (D_INNER, DT_RANK), dtype=jnp.float32, minval=-dt_init_std, maxval=dt_init_std)
        u = jax.random.uniform(ks[6], (D_INNER,), dtype=jnp.float32)
        dt = jnp.clip(jnp.exp(u * (math.log(DT_MAX) - math.log(DT_MIN)) + math.log(DT_MIN)), 0.0001)
        dt_bias = dt + jnp.log(-jnp.expm1(-dt))
        A_log = jnp.log(jnp.broadcast_to(jnp.arange(1, D_STATE + 1, dtype=jnp.float32), (D_INNER, D_STATE)))
        D = jnp.ones((D_INNER,), dtype=jnp.float32)
        W_out = jax.random.normal(ks[7], (D_MODEL, D_INNER), dtype=jnp.float32) * 0.02
        return {'hidden_states': hidden_states, 'W_in': W_in, 'conv_w': conv_w, 'conv_b': conv_b, 'W_x': W_x, 'W_dt': W_dt, 'dt_bias': dt_bias, 'A_log': A_log, 'D': D, 'W_out': W_out}
    _L0_attn_in = _L0_attn_setup()

    def _L0_ffn_setup():
        import math
        import jax, jax.numpy as jnp
        import numpy as np
        DIM = 512
        RANK = 8
        B, T = (4, 1024)

        def _orthogonal(key, n):
            a = jax.random.normal(key, (n, n), dtype=jnp.float32)
            q, r = jnp.linalg.qr(a)
            q = q * jnp.sign(jnp.diagonal(r))[None, :]
            return q
        key = jax.random.key(seed)
        kx, kf = jax.random.split(key)
        x = jax.random.normal(kx, (B, T, DIM), dtype=jnp.float32)
        fkeys = jax.random.split(kf, RANK)
        factors = jnp.stack([_orthogonal(fkeys[r], DIM) * (r + 1) ** (-0.5) for r in range(RANK)])
        bias = jnp.zeros((DIM,), dtype=jnp.float32)
        return {'x': x, 'factors': factors, 'bias': bias}
    _L0_ffn_in = _L0_ffn_setup()
    _d = {'L0_attn_hidden_states': _L0_attn_in['hidden_states'], 'L0_attn_W_in': _L0_attn_in['W_in'], 'L0_attn_conv_w': _L0_attn_in['conv_w'], 'L0_attn_conv_b': _L0_attn_in['conv_b'], 'L0_attn_W_x': _L0_attn_in['W_x'], 'L0_attn_W_dt': _L0_attn_in['W_dt'], 'L0_attn_dt_bias': _L0_attn_in['dt_bias'], 'L0_attn_A_log': _L0_attn_in['A_log'], 'L0_attn_D': _L0_attn_in['D'], 'L0_attn_W_out': _L0_attn_in['W_out'], 'L0_ffn_factors': _L0_ffn_in['factors'], 'L0_ffn_bias': _L0_ffn_in['bias']}
    _x0 = _d['L0_attn_hidden_states']
    _d['L0_attn_hidden_states'] = jax.random.normal(jax.random.fold_in(jax.random.key(seed), 1), (16, 512, 512), dtype=_x0.dtype)
    del _x0
    return _d

def reference(L0_attn_hidden_states, L0_attn_W_in, L0_attn_conv_w, L0_attn_conv_b, L0_attn_W_x, L0_attn_W_dt, L0_attn_dt_bias, L0_attn_A_log, L0_attn_D, L0_attn_W_out, L0_ffn_factors, L0_ffn_bias):

    def _L0_attn_ref(hidden_states, W_in, conv_w, conv_b, W_x, W_dt, dt_bias, A_log, D, W_out):
        import jax, jax.numpy as jnp
        import numpy as np
        import math
        D_MODEL = 512
        D_STATE = 16
        D_CONV = 4
        EXPAND = 2
        D_INNER = EXPAND * D_MODEL
        DT_RANK = math.ceil(D_MODEL / 16)
        BATCH = 2
        SEQLEN = 256
        DT_MIN, DT_MAX = (0.001, 0.1)

        def _hadamard_matrix(n):
            H = np.array([[1.0]], dtype=np.float32)
            while H.shape[0] < n:
                H = np.block([[H, H], [H, -H]])
            return H
        _H = jnp.asarray(_hadamard_matrix(D_INNER) / math.sqrt(D_INNER))

        def _selective_scan(u, delta, A, Bm, Cm, D, z):
            xs = (jnp.moveaxis(delta, 2, 0), jnp.moveaxis(u, 2, 0), jnp.moveaxis(Bm, 2, 0), jnp.moveaxis(Cm, 2, 0))
            b = u.shape[0]
            state0 = jnp.zeros((b, A.shape[0], A.shape[1]), dtype=u.dtype)

            def step(state, inp):
                dt_t, u_t, B_t, C_t = inp
                dA = jnp.exp(dt_t[:, :, None] * A[None])
                dBu = (dt_t * u_t)[:, :, None] * B_t[:, None, :]
                state = state * dA + dBu
                y_t = jnp.einsum('bdn,bn->bd', state, C_t)
                return (state, y_t)
            _, ys = jax.lax.scan(step, state0, xs)
            y = jnp.moveaxis(ys, 0, 2)
            y = y + D[None, :, None] * u
            return y * jax.nn.silu(z)
        b, l, _ = hidden_states.shape
        xz = jnp.einsum('bld,ed->bel', hidden_states, W_in)
        x, z = jnp.split(xz, 2, axis=1)
        x = jax.lax.conv_general_dilated(x, conv_w[:, None, :], window_strides=(1,), padding=[(D_CONV - 1, 0)], dimension_numbers=('NCH', 'OIH', 'NCH'), feature_group_count=D_INNER)
        x = jax.nn.silu(x + conv_b[None, :, None])
        x_dbl = jnp.einsum('bdl,ed->ble', x, W_x)
        dt_r, Bm, Cm = jnp.split(x_dbl, [DT_RANK, DT_RANK + D_STATE], axis=-1)
        delta = jnp.einsum('blr,dr->bdl', dt_r, W_dt)
        delta = jax.nn.softplus(delta + dt_bias[None, :, None])
        A = -jnp.exp(A_log)
        y = _selective_scan(x, delta, A, jnp.moveaxis(Bm, 1, 2), jnp.moveaxis(Cm, 1, 2), D, z)
        y = jnp.moveaxis(y, 1, 2)
        y = y @ _H
        return y @ W_out.T

    def _L0_ffn_ref(x, factors, bias):
        import math
        import jax, jax.numpy as jnp
        import numpy as np
        DIM = 512
        RANK = 8
        B, T = (4, 1024)

        def _orthogonal(key, n):
            a = jax.random.normal(key, (n, n), dtype=jnp.float32)
            q, r = jnp.linalg.qr(a)
            q = q * jnp.sign(jnp.diagonal(r))[None, :]
            return q
        rank = factors.shape[0]
        mixed = jnp.einsum('btd,rde->bte', x, factors)
        mixed = mixed / math.sqrt(rank) + bias
        return mixed
    x = L0_attn_hidden_states
    xn = _layernorm(x, axis=-1)
    s = _L0_attn_ref(xn, L0_attn_W_in, L0_attn_conv_w, L0_attn_conv_b, L0_attn_W_x, L0_attn_W_dt, L0_attn_dt_bias, L0_attn_A_log, L0_attn_D, L0_attn_W_out)
    g = _silu(_L0_ffn_ref(xn, L0_ffn_factors, L0_ffn_bias))
    x = x + s * g
    return x

_drawn_inputs = setup_inputs


def setup_inputs(seed=0):
    import zlib

    import numpy as np

    out = dict(_drawn_inputs(seed))
    spreads = {'L0_attn_D': (1.0, 0.2), 'L0_ffn_bias': (0.0, 0.1)}
    factors = {}
    for name, (base, spread) in spreads.items():
        noise = np.random.default_rng([zlib.crc32(name.encode()), seed]).standard_normal(out[name].shape)
        drawn = base * np.exp(spread * noise) if base else spread * noise
        out[name] = jnp.asarray(drawn.astype(out[name].dtype))
    for name, factor in factors.items():
        out[name] = (out[name] * factor).astype(out[name].dtype)
    return out
```

```python
from contextlib import ExitStack

import numpy as np

import concourse.bass as bass
from concourse import mybir

F32 = mybir.dt.float32
ALU = mybir.AluOpType
ACT = mybir.ActivationFunctionType

APART = (mybir.EngineType.Activation, mybir.EngineType.Pool, mybir.EngineType.SP)
P = 128
BATCH, TOK, DM = 16, 512, 512
DI = 2 * DM
NS = 16
TAPS = 4
RANK = DM // 16
FACTORS = 8
KT = DM // P
DT = DI // P
TT = TOK // P
HALF = DT // 2
STEPS = 2 * NS
PAIRS = 2 * STEPS
MACS = TT * STEPS
NX = RANK + 2 * NS
EPS = 1e-5

X_TILE = [2 * i for i in range(DT)]
X_PROJ = 17
C_TURN = 19
DT_TILE = [20 + i for i in range(DT)]
NORM = [28 + j for j in range(TT)]
Z_TILE = [2 * i + 1 for i in range(DT)]
Y_TURN = [2 * i + 2 for i in range(DT)]
FFN = [17 + j for j in range(TT)]
OUT = [21 + 2 * j for j in range(TT)]
LAST = 32


class Count:

    def __init__(self, sem, per, unit, waited):
        self.sem, self.per, self.unit, self.waited = sem, per, unit, waited

    def upto(self, batch, n):
        if isinstance(batch, int):
            return (batch * self.per + n) * self.unit
        return batch * (self.per * self.unit) + n * self.unit


def wait(e, count, batch, n, apart=False):
    value = count.upto(batch, n)
    if not isinstance(value, int) or value > 0:
        e.wait_ge(count.sem, value)
        if not isinstance(value, int) and (apart or e.engine in APART):
            e.sem_inc(count.waited, 1)


class Slots:

    def __init__(self):
        self.at = {}

    def put(self, step, position, task):
        self.at.setdefault(step, []).append((position, task))

    def run(self, step, own):
        extra = sorted(self.at.get(step, []), key=lambda x: x[0])
        for i, instruction in enumerate(own):
            while extra and extra[0][0] <= i:
                extra.pop(0)[1]()
            instruction()
        for _, task in extra:
            task()


def program(nc, x, w_in, w_x, w_dt, w_out, a_log, conv_w, chan, factors, bias, had, ident_in,
            u_dram, xn_dram, b_dram, out):
    ctx = ExitStack()
    with ctx:
        def sb(name, shape):
            return ctx.enter_context(nc.sbuf_tensor(name, shape, F32))

        def ps(name, shape):
            return ctx.enter_context(nc.psum_tensor(name, shape, F32))

        waited = ctx.enter_context(nc.semaphore("waited"))

        def count(name, per, unit=1):
            return Count(ctx.enter_context(nc.semaphore(name)), per, unit, waited)

        wx_sb = sb("wx_sb", [P, DT, NX])
        wdt_sb = sb("wdt_sb", [RANK + 1, DI])
        wc_sb = sb("wc_sb", [P, DT, DM])
        f_sb = sb("f_sb", [P, KT, DM])
        ident = sb("ident", [P, P])
        a_sb = sb("a_sb", [P, DT * NS])
        cw = sb("cw", [P, DT * TAPS])
        ch = sb("ch", [P, 3, DT])
        bias_sb = wdt_sb[RANK:RANK + 1, 0:DM]
        ones = wdt_sb[RANK:RANK + 1, DM:DM + P]
        w_xt = [sb(f"w_xt{i}", [P, KT, P]) for i in range(2)]
        w_zt = [sb(f"w_zt{i}", [P, KT, P]) for i in range(2)]
        delta = sb("delta", [P, 2, DT, TOK])
        dtu = sb("dtu", [P, 2, DT, TOK])
        acc = sb("acc", [P, DT, TT, P])
        acc_f = sb("acc_f", [P, DT, TT, P])
        h = [sb(f"h{i}", [P, HALF, TOK]) for i in range(2)]
        dbu = [sb(f"dbu{i}", [P, 2, TOK]) for i in range(2)]
        b_rep = [sb(f"b_rep{i}", [P, TOK]) for i in range(2)]
        c_now = sb("c_now", [P, TT, NS])
        c_next = sb("c_next", [P, TT, NS])
        xnt = sb("xnt", [P, KT, TOK])
        xnt_b = sb("xnt_b", [P, KT, TOK])
        x_in = [buf[:, :, :].rearrange("p a b -> p (a b)") for buf in w_xt + w_zt]
        stats = sb("stats", [P, 2, 6])
        mv = sb("mv", [P, 2, 2])
        rs = sb("rs", [P, 2, 2])
        power = sb("power", [P, 1])
        side = [sb(f"side{i}", [P, TOK]) for i in range(2)]
        sp = [sb(f"sp{i}", [P, TOK]) for i in range(2)]
        sz = sb("sz", [P, TOK])
        yb = sb("yb", [P, TOK])
        ob = [sz, yb]
        ident_had = sz[:, 0:P]
        gf = sb("gf", [P, TT, DM])
        xdbl = sb("xdbl", [NX, TOK])

        decay = [ps(f"decay{i}", [P, 2, TOK]) for i in range(2)]
        ht = [ps(f"ht{i}", [P, HALF, P]) for i in range(2)]
        pf = ps("pf", [P, TOK])
        pb = ps("pb", [P, TOK])

        n_decay = count("n_decay", PAIRS)
        n_dbu = count("n_dbu", PAIRS)
        n_scan = count("n_scan", PAIRS)
        n_ht = count("n_ht", MACS)
        n_mac = count("n_mac", MACS)
        n_brep = [count(f"n_brep{i}", NS // 2, 16) for i in range(2)]
        n_xin = [count(f"n_xin{j}", 1, 16) for j in range(TT)]
        n_stat = count("n_stat", 3 * TT)
        n_shift = count("n_shift", TT)
        n_rstd = count("n_rstd", TT)
        n_norm = count("n_norm", TT)
        n_xturn = count("n_xturn", TT)
        n_xnt = count("n_xnt", TT)
        n_xspill = count("n_xspill", 1, 16)
        n_wx = [count(f"n_wx{i}", DT // 2, 16) for i in range(2)]
        n_in = count("n_in", DT)
        n_tap0 = count("n_tap0", DT)
        n_tap = count("n_tap", DT * (TAPS - 1))
        n_tanh = count("n_tanh", DT)
        n_u = count("n_u", DT)
        n_uspill = count("n_uspill", DT, 16)
        n_xproj = count("n_xproj", 1)
        n_xdbl = count("n_xdbl", 1)
        n_bspill = count("n_bspill", 1, 16)
        n_cturn = count("n_cturn", 1)
        n_cnext = count("n_cnext", 1)
        n_cnow = count("n_cnow", 1)
        n_dt = count("n_dt", DT)
        n_relu = count("n_relu", DT)
        n_abs = count("n_abs", DT)
        n_exp = count("n_exp", DT)
        n_ln = count("n_ln", DT)
        n_delta = count("n_delta", DT)
        n_dtu = count("n_dtu", DT)
        n_xback = count("n_xback", 1, 16)
        n_wz = [count(f"n_wz{i}", DT // 2, 16) for i in range(2)]
        n_z = count("n_z", DT)
        n_ztanh = count("n_ztanh", DT)
        n_sz = count("n_sz", DT)
        n_side = [count(f"n_side{i}", (DT + TT) // 2, 16) for i in range(2)]
        n_yturn = count("n_yturn", DT)
        n_y = count("n_y", DT)
        n_g = count("n_g", DT)
        n_ffn = count("n_ffn", TT)
        n_ftanh = count("n_ftanh", TT)
        n_gf = count("n_gf", TT)
        n_out = count("n_out", TT)
        n_o = count("n_o", TT)
        n_sum = count("n_sum", TT)
        n_store = [count(f"n_store{i}", TT // 2, 16) for i in range(2)]
        p_load = count("p_load", 1, 16)
        p_wout = count("p_wout", 1, 16)
        p_f = [count(f"p_f{i}", 1, 16) for i in range(FACTORS)]
        p_fadd = count("p_fadd", 1)
        p_fscale = count("p_fscale", 1)
        p_act = count("p_act", 1)
        p_dve = count("p_dve", 1)
        p_h = count("p_h", 1)
        p_hcopy = count("p_hcopy", 1)
        p_fold = count("p_fold", 1)

        LOADS = 8
        f_part = [f_sb] + [buf[:, 1, i * KT:(i + 1) * KT, :] for buf in (delta, dtu) for i in range(2)]

        def f_slot(r):
            return f_sb[:, :, :] if r == 0 else f_part[1 + (r - 1) % 4]

        def turn(b):
            return b % 2

        block = ctx.enter_context(nc.Block())

        def rounds(e, round_):
            round_(0, True, True, False)
            round_(1, True, True, True)
            with e.Fori(2, BATCH - 2) as t:
                round_(t, True, True, True)
            round_(BATCH - 2, True, False, True)
            round_(BATCH - 1, False, False, True)

        @block.tensor
        def _(e):
            def turns(b, s, j):
                def task():
                    wait(e, n_scan, b, 2 * s + 2)
                    wait(e, n_mac, b, TT * s + j - 1)
                    for i in range(HALF):
                        mm = e.transpose(ht[j % 2][:, i, :], h[s % 2][:, i, j * P:(j + 1) * P], ident[:, :])
                    mm.then_inc(n_ht.sem, 1)
                return task

            def norm(q, b):
                for j in range(TT):
                    def task(j=j):
                        wait(e, n_norm, b, j + 1)
                        if j == 0:
                            wait(e, n_abs, b, 0)
                        else:
                            wait(e, n_xnt, b, j)
                        for k in range(KT):
                            mm = e.transpose(pf[:, k * P:(k + 1) * P], x_in[j][:, k * P:(k + 1) * P], ident[:, :])
                        mm.then_inc(n_xturn.sem, 1)
                    q.put(NORM[j], 3, task)

            def front(q, b):
                for i in range(DT):
                    def x_tile(k, i=i):
                        if k == 0:
                            wait(e, n_xnt, b, TT)
                            wait(e, n_u, b, i)
                            wait(e, n_wx[i % 2], b, i // 2 + 1)
                        mm = e.matmul(pf[:, :], w_xt[i % 2][:, k, :], xnt[:, k, :], start=k == 0, stop=k == KT - 1)
                        if k == KT - 1:
                            mm.then_inc(n_in.sem, 1)
                    for k in range(KT):
                        q.put(X_TILE[i], 3 + k // 2, lambda k=k, f=x_tile: f(k))

                def x_proj(i):
                    if i == 0:
                        wait(e, n_u, b, DT)
                    mm = e.matmul(pf[0:NX, :], wx_sb[:, i, :], dtu[:, turn(b), i, :], start=i == 0, stop=i == DT - 1)
                    if i == DT - 1:
                        mm.then_inc(n_xproj.sem, 1)
                for i in range(DT):
                    q.put(X_PROJ + i // 4, 1 + i % 4, lambda i=i: x_proj(i))

                def c_turn():
                    wait(e, n_xdbl, b, 1, apart=True)
                    for j in range(TT):
                        mm = e.transpose(pf[:, j * NX:(j + 1) * NX], xdbl[:, j * P:(j + 1) * P], ident[0:NX, 0:NX])
                    mm.then_inc(n_cturn.sem, 1)
                q.put(C_TURN, 3, c_turn)

                for i in range(DT):
                    def dt_tile(i=i):
                        if i == 0:
                            wait(e, n_cnext, b, 1)
                        else:
                            wait(e, n_abs, b, i)
                            wait(e, n_relu, b, i)
                        e.matmul(pf[:, :], wdt_sb[0:RANK, i * P:(i + 1) * P], xdbl[0:RANK, :],
                                 start=True, stop=True).then_inc(n_dt.sem, 1)
                    q.put(DT_TILE[i], 3, dt_tile)

            def back(q, b):
                for i in range(DT):
                    def z_tile(k, i=i):
                        if k == 0:
                            wait(e, n_xback, b, 1)
                            if i == 0:
                                wait(e, n_o, b, 0)
                            else:
                                wait(e, n_y, b, i)
                            wait(e, n_wz[i % 2], b, i // 2 + 1)
                        mm = e.matmul(pb[:, :], w_zt[i % 2][:, k, :], xnt_b[:, k, :], start=k == 0, stop=k == KT - 1)
                        if k == KT - 1:
                            mm.then_inc(n_z.sem, 1)
                    for k in range(KT):
                        q.put(Z_TILE[i], 2 + k // 2, lambda k=k, f=z_tile: f(k))

                    def y_turn(i=i):
                        wait(e, n_mac, b, MACS)
                        wait(e, n_sz, b, i + 1)
                        for j in range(TT):
                            mm = e.transpose(pb[:, j * P:(j + 1) * P], acc_f[:, i, j, :], ident[:, :])
                        mm.then_inc(n_yturn.sem, 1)
                    q.put(Y_TURN[i], 3, y_turn)

                for j in range(TT):
                    def ffn(k, j=j):
                        if k == 0:
                            wait(e, n_y, b, DT)
                            if j:
                                wait(e, n_gf, b, j)
                        e.matmul(pb[:, :], xnt_b[:, k, j * P:(j + 1) * P], f_sb[:, k, :], start=k == 0, stop=False)
                        if k == KT - 1:
                            e.matmul(pb[:, :], ones, bias_sb, start=False, stop=True).then_inc(n_ffn.sem, 1)
                    for k in range(KT):
                        q.put(FFN[j], 2 + k // 2, lambda k=k, f=ffn: f(k))

                    def out_tile(i, j=j):
                        if i == 0:
                            wait(e, n_g, b, DT)
                            if j == 0:
                                wait(e, n_gf, b, TT)
                            else:
                                wait(e, n_o, b, j)
                        g = acc_f[:, i, :, :].rearrange("p a b -> p (a b)")
                        mm = e.matmul(pb[:, :], g[:, j * P:(j + 1) * P], wc_sb[:, i, :], start=i == 0, stop=i == DT - 1)
                        if i == DT - 1:
                            mm.then_inc(n_out.sem, 1)
                    for i in range(DT):
                        q.put(OUT[j] + i // 4, 1 + i % 4, lambda i=i, f=out_tile: f(i))

            wait(e, p_load, 0, LOADS)
            q = Slots()
            norm(q, 0)
            for s in range(LAST):
                q.run(s, [])
            wait(e, p_wout, 0, 2)
            for i in range(DT):
                bank = (decay[0][:, 0, :], decay[0][:, 1, :], decay[1][:, 0, :], decay[1][:, 1, :])[i % 4]
                if i >= 4:
                    wait(e, p_hcopy, 0, i - 3)
                e.matmul(bank, ident_had, acc[:, i, :, :].rearrange("p a b -> p (a b)"),
                         start=True, stop=True).then_inc(p_h.sem, 1)
            q = Slots()
            front(q, 0)
            norm(q, 1)
            for s in range(LAST):
                q.run(s, [])

            def round_(t, has_front, has_norm, has_back):
                q = Slots()
                if has_front:
                    front(q, t + 1)
                if has_norm:
                    norm(q, t + 2)
                if has_back:
                    back(q, t - 1)
                for s in range(STEPS):
                    if s == 0:
                        own = [turns(t - 1, STEPS - 1, j) for j in range(TT)] if has_back else []
                    else:
                        own = [turns(t, s - 1, j) for j in range(TT)]
                    q.run(s, own)

            wait(e, p_fold, 0, 24)
            wait(e, p_fscale, 0, 1)
            rounds(e, round_)
            for j in range(TT):
                turns(BATCH - 1, STEPS - 1, j)()
            q = Slots()
            back(q, BATCH - 1)
            for s in range(LAST):
                q.run(s, [])

        @block.scalar
        def _(e):
            def decays(b, s, p, i):
                q, tile = 2 * s + p, HALF * (s % 2) + 2 * p + i

                def task():
                    if i == 0:
                        if s == 0 and p == 0:
                            wait(e, n_delta, b, DT)
                        wait(e, n_scan, b, q - 1)
                    n = tile * NS + s // 2
                    op = e.activation(decay[q % 2][:, i, 1:TOK], delta[:, turn(b), tile, 1:TOK], ACT.Exp,
                                      bias=0.0, scale=a_sb[:, n:n + 1])
                    if i == 1:
                        op.then_inc(n_decay.sem, 1)
                return task

            def norm(q, b):
                for j in range(TT):
                    def normalise(j=j):
                        wait(e, n_shift, b, j + 1)
                        e.activation(x_in[j], x_in[j], ACT.Identity, bias=rs[:, j % 2, 1:2],
                                     scale=rs[:, j % 2, 0:1]).then_inc(n_norm.sem, 1)
                    q.put(NORM[j] - 1, 3, normalise)

                    def evacuate(j=j):
                        wait(e, n_xturn, b, j + 1)
                        if j == 0:
                            wait(e, n_in, b, 0)
                            wait(e, n_xspill, b, 0)
                        e.copy(xnt[:, :, j * P:(j + 1) * P],
                               pf[:, :].rearrange("p (k b) -> p k b", k=KT)).then_inc(n_xnt.sem, 1)
                    q.put(NORM[j], 9, evacuate)

            def front(q, b):
                for i in range(DT):
                    def tap0(i=i):
                        if i == 0:
                            wait(e, n_dbu, b - 1, 0) if not isinstance(b, int) or b >= 1 else None
                        wait(e, n_in, b, i + 1)
                        k = i * TAPS + TAPS - 1
                        e.activation(dtu[:, turn(b), i, :], pf[:, :], ACT.Identity, bias=ch[:, 0, i:i + 1],
                                     scale=cw[:, k:k + 1]).then_inc(n_tap0.sem, 1)
                    q.put(X_TILE[i] + 1, 1, tap0)

                    def tanh(i=i):
                        wait(e, n_tap, b, (TAPS - 1) * (i + 1))
                        e.activation(pf[:, :], dtu[:, turn(b), i, :], ACT.Tanh).then_inc(n_tanh.sem, 1)
                    q.put(X_TILE[i] + 2, 1, tanh)

                def take_xdbl():
                    wait(e, n_xproj, b, 1)
                    wait(e, n_dt, b, 0)
                    wait(e, n_bspill, b, 0)
                    e.copy(xdbl[:, :], pf[0:NX, :]).then_inc(n_xdbl.sem, 1)
                q.put(X_PROJ + 2, 1, take_xdbl)

                for i in range(DT):
                    def relu(i=i):
                        wait(e, n_dt, b, i + 1)
                        e.activation(delta[:, turn(b), i, :], pf[:, :], ACT.Relu, bias=ch[:, 1, i:i + 1],
                                     scale=1.0).then_inc(n_relu.sem, 1)
                        if i >= 2:
                            wait(e, n_delta, b, i - 1)
                        elif i == 1 and not (isinstance(b, int) and b < 2):
                            wait(e, n_gf, b - 1, 0)
                        e.activation(sp[(i + 1) % 2][:, :], pf[:, :], ACT.Abs, bias=ch[:, 1, i:i + 1],
                                     scale=1.0).then_inc(n_abs.sem, 1)
                    q.put(DT_TILE[i] + 1, 1, relu)

                    def exp(i=i):
                        wait(e, n_abs, b, i + 1)
                        e.activation(sp[(i + 1) % 2][:, :], sp[(i + 1) % 2][:, :], ACT.Exp, scale=-1.0).then_inc(n_exp.sem, 1)
                    q.put(DT_TILE[i] + 1, 2, exp)

                    def ln(i=i):
                        wait(e, n_exp, b, i + 1)
                        e.activation(sp[(i + 1) % 2][:, :], sp[(i + 1) % 2][:, :], ACT.Ln, bias=1.0).then_inc(n_ln.sem, 1)
                    q.put(DT_TILE[i] + 1, 3, ln)

            def back(q, b):
                for i in range(DT):
                    def z_tanh(i=i):
                        if i == 0:
                            wait(e, n_delta, b + 1, DT) if not isinstance(b, int) or b < BATCH - 1 else None
                        wait(e, n_z, b, i + 1)
                        e.activation(sp[0][:, :], pb[:, :], ACT.Tanh, scale=0.5).then_inc(n_ztanh.sem, 1)
                    q.put(Z_TILE[i] + 1, 1, z_tanh)
                for j in range(TT):
                    def f_tanh(j=j):
                        wait(e, n_ffn, b, j + 1)
                        e.activation(sp[0][:, :], pb[:, :], ACT.Tanh, scale=0.5).then_inc(n_ftanh.sem, 1)
                    q.put(FFN[j] + 1, 1, f_tanh)

            wait(e, p_load, 0, LOADS)
            e.activation(a_sb[:, :], a_sb[:, :], ACT.Exp).then_inc(p_act.sem, 1)
            e.mul(cw[:, :], cw[:, :], 0.5).then_inc(p_act.sem, 1)
            e.mul(ch[:, 0, :], ch[:, 0, :], 0.5).then_inc(p_act.sem, 1)
            wait(e, p_act, 0, 1)
            e.mul(a_sb[:, :], a_sb[:, :], -1.0).then_inc(p_act.sem, 1)
            wait(e, p_act, 0, 4)
            q = Slots()
            norm(q, 0)
            for s in range(LAST):
                q.run(s, [])
            for i in range(DT):
                bank = (decay[0][:, 0, :], decay[0][:, 1, :], decay[1][:, 0, :], decay[1][:, 1, :])[i % 4]
                wait(e, p_h, 0, i + 1)
                e.copy(acc_f[:, i, :, :], bank.rearrange("p (a b) -> p a b", a=TT)).then_inc(p_hcopy.sem, 1)
            q = Slots()
            front(q, 0)
            norm(q, 1)
            for s in range(LAST):
                q.run(s, [])
            wait(e, p_fadd, 0, FACTORS - 1)
            e.mul(f_sb[:, :, :], f_sb[:, :, :], FACTORS ** -0.5).then_inc(p_fscale.sem, 1)
            wait(e, p_dve, 0, 2)

            def round_(t, has_front, has_norm, has_back):
                q = Slots()
                if has_front:
                    front(q, t + 1)
                if has_norm:
                    norm(q, t + 2)
                if has_back:
                    back(q, t - 1)
                for s in range(STEPS):
                    q.run(s, [decays(t, s, p, i) for p in range(2) for i in range(2)])

            rounds(e, round_)
            q = Slots()
            back(q, BATCH - 1)
            for s in range(LAST):
                q.run(s, [])

        @block.gpsimd
        def _(e):
            def inputs(b, s, p):
                q, tile = 2 * s + p, HALF * (s % 2) + 2 * p
                n = s // 2

                def task():
                    if s == 0 and p == 0:
                        wait(e, n_dtu, b, DT)
                    wait(e, n_brep[n % 2], b, n // 2 + 1)
                    wait(e, n_scan, b, q - 1)
                    e.tensor_tensor(dbu[q % 2][:, :, :], dtu[:, turn(b), tile:tile + 2, :],
                                    b_rep[n % 2][:, None, :].broadcast_to([P, 2, TOK]), ALU.mult).then_inc(n_dbu.sem, 1)
                return task

            def front(q, b):
                for i in range(DT):
                    def add(i=i):
                        wait(e, n_ln, b, i + 1)
                        e.tensor_tensor(delta[:, turn(b), i, :], delta[:, turn(b), i, :], sp[(i + 1) % 2][:, :],
                                        ALU.add).then_inc(n_delta.sem, 1)
                    q.put(DT_TILE[i] + 2, 0, add)

                    def mult(i=i):
                        wait(e, n_delta, b, i + 1)
                        if i == 0:
                            wait(e, n_uspill, b, DT)
                            wait(e, n_xproj, b, 1)
                        e.tensor_tensor(dtu[:, turn(b), i, :], dtu[:, turn(b), i, :], delta[:, turn(b), i, :],
                                        ALU.mult).then_inc(n_dtu.sem, 1)
                    q.put(DT_TILE[i] + 2, 1, mult)

            def back(q, b):
                for i in range(DT):
                    def gate(i=i):
                        wait(e, n_y, b, i + 1)
                        wait(e, n_sz, b, i + 1)
                        e.tensor_tensor(acc_f[:, i, :, :].rearrange("p a b -> p (a b)"), yb[:, :], sz[:, :],
                                        ALU.mult).then_inc(n_g.sem, 1)
                    q.put(Y_TURN[i] + 1, 1, gate)
                for j in range(TT):
                    def residual(j=j):
                        wait(e, n_o, b, j + 1)
                        wait(e, n_side[j % 2], b, (DT + j) // 2 + 1)
                        e.tensor_tensor(ob[j % 2][:, :], ob[j % 2][:, :], side[j % 2][:, :],
                                        ALU.add).then_inc(n_sum.sem, 1)
                    q.put(OUT[j] + 2, 1, residual)

            def norm(q, b):
                for j in range(TT):
                    def rstd(j=j, r=j % 2):
                        wait(e, n_stat, b, 3 * j + 3)
                        if j >= 2:
                            wait(e, n_norm, b, j - 1)
                        else:
                            wait(e, n_norm, b, 0)
                        e.tensor_tensor(rs[:, r, 0:1], mv[:, r, 1:2], power[:, :], ALU.pow).then_inc(n_rstd.sem, 1)
                    q.put(NORM[j] - 2, 9, rstd)

            wait(e, p_dve, 0, 1)
            q = Slots()
            norm(q, 0)
            for s in range(LAST):
                q.run(s, [])
            def add_factors(rs_):
                for r in rs_:
                    wait(e, p_f[0], 0, 1)
                    wait(e, p_f[r], 0, 1)
                    wait(e, p_fadd, 0, r - 1)
                    e.tensor_tensor(f_sb[:, :, :], f_sb[:, :, :], f_slot(r), ALU.add).then_inc(p_fadd.sem, 1)

            add_factors(range(1, 5))
            q = Slots()
            front(q, 0)
            norm(q, 1)
            for s in range(LAST):
                q.run(s, [])
            add_factors(range(5, FACTORS))

            def round_(t, has_front, has_norm, has_back):
                q = Slots()
                if has_front:
                    front(q, t + 1)
                if has_norm:
                    norm(q, t + 2)
                if has_back:
                    back(q, t - 1)
                for s in range(STEPS):
                    q.run(s, [inputs(t, s, p) for p in range(2)])

            rounds(e, round_)
            q = Slots()
            back(q, BATCH - 1)
            for s in range(LAST):
                q.run(s, [])

        @block.vector
        def _(e):
            def scan(b, s, p):
                q = 2 * s + p

                def task():
                    wait(e, n_decay, b, q + 1)
                    wait(e, n_dbu, b, q + 1)
                    e.tensor_tensor_scan(h[s % 2][:, 2 * p:2 * p + 2, :].rearrange("p a b -> p (a b)"),
                                         decay[q % 2][:, :, :].rearrange("p a b -> p (a b)"),
                                         dbu[q % 2][:, :, :].rearrange("p a b -> p (a b)"),
                                         0.0, ALU.mult, ALU.add).then_inc(n_scan.sem, 1)
                return task

            def mac(b, s, j):
                n, half = s // 2, s % 2

                def task():
                    tiles = slice(half * HALF, (half + 1) * HALF)
                    wait(e, n_ht, b, TT * s + j + 1)
                    if s == 0 and j == 0:
                        wait(e, n_cnow, b, 1)
                    c = c_now[:, j, n:n + 1]
                    if n == 0:
                        op = e.tensor_scalar(acc[:, tiles, j, :], ht[j % 2][:, :, :], c, None, ALU.mult)
                    else:
                        wait(e, n_mac, b, TT * (s - 2) + j + 1)
                        if n == NS - 1 and half == 0 and j == 0:
                            wait(e, n_out, b, 0)
                        to = acc_f if n == NS - 1 else acc
                        op = e.scalar_tensor_tensor(out=to[:, tiles, j, :], in0=ht[j % 2][:, :, :], scalar=c,
                                                    in1=acc[:, tiles, j, :], op0=ALU.mult, op1=ALU.add)
                    op.then_inc(n_mac.sem, 1)
                return task

            def norm(q, b):
                for j in range(TT):
                    r = j % 2

                    def bn(j=j, r=r):
                        wait(e, n_xin[j], b, 1)
                        e.bn_stats(stats[:, r, :], x_in[j]).then_inc(n_stat.sem, 1)

                    def aggr(j=j, r=r):
                        wait(e, n_stat, b, 3 * j + 1, apart=True)
                        e.bn_aggr(mv[:, r, :], stats[:, r, :]).then_inc(n_stat.sem, 1)

                    def eps(j=j, r=r):
                        wait(e, n_stat, b, 3 * j + 2)
                        if j >= 2:
                            wait(e, n_norm, b, j - 1)
                        else:
                            wait(e, n_norm, b, 0)
                        e.tensor_scalar(mv[:, r, 1:2], mv[:, r, 1:2], EPS, None, ALU.add).then_inc(n_stat.sem, 1)

                    def shift(j=j, r=r):
                        wait(e, n_rstd, b, j + 1)
                        e.tensor_scalar(rs[:, r, 1:2], mv[:, r, 0:1], rs[:, r, 0:1], -1.0, ALU.mult,
                                        ALU.mult).then_inc(n_shift.sem, 1)
                    for k, f in enumerate((bn, aggr, eps)):
                        q.put(NORM[j] - 2, 2 * k, f)
                    q.put(NORM[j] - 1, 1, shift)

            def front(q, b):
                for i in range(DT):
                    for k in range(1, TAPS):
                        def tap(i=i, k=k):
                            w = cw[:, i * TAPS + TAPS - 1 - k:i * TAPS + TAPS - k]
                            v = dtu[:, turn(b), i, k:TOK]
                            wait(e, n_tap0, b, i + 1)
                            wait(e, n_tap, b, (TAPS - 1) * i + k - 1)
                            e.scalar_tensor_tensor(out=v, in0=pf[:, 0:TOK - k], scalar=w, in1=v, op0=ALU.mult,
                                                   op1=ALU.add).then_inc(n_tap.sem, 1)
                        q.put(X_TILE[i] + 1, 2 * k, tap)

                    def silu(i=i):
                        wait(e, n_tanh, b, i + 1)
                        e.scalar_tensor_tensor(out=dtu[:, turn(b), i, :], in0=pf[:, :], scalar=1.0,
                                               in1=dtu[:, turn(b), i, :], op0=ALU.add, op1=ALU.mult).then_inc(n_u.sem, 1)
                    q.put(X_TILE[i] + 2, 2, silu)

                def take_c():
                    wait(e, n_cturn, b, 1)
                    wait(e, n_cnow, b, 0)
                    e.tensor_copy(c_next[:, :, :], pf[:, 0:TT * NX].rearrange("p (j x) -> p j x", j=TT)
                                  [:, :, RANK + NS:NX]).then_inc(n_cnext.sem, 1)
                q.put(C_TURN + 1, 1, take_c)

            def take_over(b):
                def task():
                    wait(e, n_cnext, b, 1)
                    wait(e, n_mac, b, 0)
                    e.tensor_copy(c_now[:, :, :], c_next[:, :, :]).then_inc(n_cnow.sem, 1)
                return task

            def back(q, b):
                for i in range(DT):
                    def silu_z(i=i):
                        wait(e, n_ztanh, b, i + 1)
                        wait(e, n_g, b, i)
                        if i == 0:
                            wait(e, n_store[0], b, 0)
                        e.scalar_tensor_tensor(out=sz[:, :], in0=sp[0][:, :], scalar=1.0, in1=pb[:, :], op0=ALU.add,
                                               op1=ALU.mult).then_inc(n_sz.sem, 1)
                    q.put(Z_TILE[i] + 1, 2, silu_z)

                    def skip(i=i):
                        wait(e, n_yturn, b, i + 1)
                        wait(e, n_side[i % 2], b, i // 2 + 1)
                        wait(e, n_g, b, i)
                        if i == 0:
                            wait(e, n_store[1], b, 0)
                        e.scalar_tensor_tensor(out=yb[:, :], in0=side[i % 2][:, :], scalar=ch[:, 2, i:i + 1],
                                               in1=pb[:, :], op0=ALU.mult, op1=ALU.add).then_inc(n_y.sem, 1)
                    q.put(Y_TURN[i] + 1, 1, skip)
                for j in range(TT):
                    def silu_f(j=j):
                        wait(e, n_ftanh, b, j + 1)
                        e.scalar_tensor_tensor(out=gf[:, j, :], in0=sp[0][:, :], scalar=1.0, in1=pb[:, :], op0=ALU.add,
                                               op1=ALU.mult).then_inc(n_gf.sem, 1)
                    q.put(FFN[j] + 1, 2, silu_f)

                    def gate(j=j):
                        wait(e, n_out, b, j + 1)
                        if j >= 2:
                            wait(e, n_store[j % 2], b, j // 2)
                        else:
                            wait(e, n_g, b, DT)
                        wait(e, n_gf, b, j + 1)
                        e.tensor_tensor(ob[j % 2][:, :], pb[:, :], gf[:, j, :], ALU.mult).then_inc(n_o.sem, 1)
                    q.put(OUT[j] + 2, 0, gate)

            e.memset(ones, 1.0)
            e.memset(power[:, :], -0.5).then_inc(p_dve.sem, 1)
            q = Slots()
            norm(q, 0)
            for s in range(LAST):
                q.run(s, [])
            q = Slots()
            front(q, 0)
            norm(q, 1)
            for s in range(LAST):
                q.run(s, [])
            flat = [t[:, :, :, :].rearrange("p d a b -> p d (a b)") for t in (acc_f, acc)]
            stage_from, stage_to = (flat[0], flat[1], flat[0]), (flat[1], flat[0], wc_sb)
            wait(e, p_hcopy, 0, DT)
            wait(e, p_h, 0, DT)
            for k in range(3):
                src, dst, d = stage_from[k], stage_to[k], 1 << k
                if k:
                    wait(e, p_fold, 0, DT * k)
                for i in range(DT):
                    lo, hi = i & ~d, i | d
                    e.tensor_tensor(dst[:, i, :], src[:, lo, :], src[:, hi, :],
                                    ALU.subtract if i & d else ALU.add).then_inc(p_fold.sem, 1)
            for k in range(2):
                op = e.memset(decay[k][:, :, 0:1], 0.0)
            op.then_inc(p_dve.sem, 1)

            def round_(t, has_front, has_norm, has_back):
                q = Slots()
                if has_front:
                    front(q, t + 1)
                if has_norm:
                    norm(q, t + 2)
                if has_back:
                    back(q, t - 1)
                for s in range(STEPS):
                    if s == 0:
                        macs = [mac(t - 1, STEPS - 1, j) for j in range(TT)] if has_back else []
                    else:
                        macs = [mac(t, s - 1, j) for j in range(TT)]
                    own = [scan(t, s, 0)] + macs[:2] + [scan(t, s, 1)] + macs[2:]
                    if s == 1:
                        own = [take_over(t)] + own
                    q.run(s, own)

            rounds(e, round_)
            for j in range(TT):
                mac(BATCH - 1, STEPS - 1, j)()
            q = Slots()
            back(q, BATCH - 1)
            for s in range(LAST):
                q.run(s, [])

        @block.sync
        def _(e):
            def b_load(b, n):
                def task():
                    if n == 0:
                        wait(e, n_bspill, b, 1)
                    wait(e, n_dbu, b, 4 * (n - 1) if n >= 2 else 4 * (n - 1))
                    src = b_dram[b, n:n + 1, :].broadcast_to([P, TOK])
                    e.dma_start(b_rep[n % 2][:, :], src).then_inc(n_brep[n % 2].sem, 16)
                return task

            def norm(q, b):
                for j in range(TT):
                    def load(j=j):
                        if j < 2:
                            wait(e, n_in, b, 0)
                        elif not isinstance(b, int) or b > 2:
                            wait(e, n_z, b - 2, 0)
                        e.dma_start(x_in[j], x[b, j * P:(j + 1) * P, :]).then_inc(n_xin[j].sem, 16)
                    q.put(NORM[j] - 3, 0, load)

                def spill():
                    wait(e, n_xnt, b, TT)
                    e.dma_start(xn_dram[b], xnt[:, :, :].rearrange("p a b -> p (a b)")).then_inc(n_xspill.sem, 16)
                q.put(NORM[-1], 9, spill)

            def front(q, b):
                for i in range(DT):
                    def load(i=i):
                        if i < 2:
                            wait(e, n_xturn, b, TT)
                        else:
                            wait(e, n_in, b, i - 1)
                        e.dma_start(w_xt[i % 2][:, :, :].rearrange("p a b -> p (a b)"), w_in[i]).then_inc(n_wx[i % 2].sem, 16)
                    q.put(max(0, X_TILE[i] - 2), 0, load)

                    def spill(i=i):
                        wait(e, n_u, b, i + 1)
                        e.dma_start(u_dram[b, i], dtu[:, turn(b), i, :]).then_inc(n_uspill.sem, 16)
                    q.put(X_TILE[i] + 2, 9, spill)

                def spill_b():
                    wait(e, n_xdbl, b, 1)
                    e.dma_start(b_dram[b], xdbl[RANK:RANK + NS, :]).then_inc(n_bspill.sem, 16)
                q.put(C_TURN, 9, spill_b)

            def back(q, b):
                def load_xn():
                    wait(e, n_xspill, b, 1)
                    wait(e, n_ffn, b, 0)
                    e.dma_start(xnt_b[:, :, :].rearrange("p a b -> p (a b)"), xn_dram[b]).then_inc(n_xback.sem, 16)
                q.put(0, 0, load_xn)
                for i in range(DT):
                    def load(i=i):
                        if i < 2:
                            wait(e, n_xturn, b + 3 if not isinstance(b, int) else min(b + 3, BATCH), 0)
                        else:
                            wait(e, n_z, b, i - 1)
                        e.dma_start(w_zt[i % 2][:, :, :].rearrange("p a b -> p (a b)"), w_in[DT + i]).then_inc(n_wz[i % 2].sem, 16)
                    q.put(max(0, Z_TILE[i] - 2), 1, load)

                    def side_u(i=i):
                        if i == 0:
                            wait(e, n_uspill, b, DT)
                            wait(e, n_sum, b, 0)
                        if i >= 2:
                            wait(e, n_y, b, i - 1)
                        e.dma_start(side[i % 2][:, :], u_dram[b, i]).then_inc(n_side[i % 2].sem, 16)
                    q.put(Z_TILE[i], 2, side_u)
                for j in range(TT):
                    def side_x(j=j):
                        if j < 2:
                            wait(e, n_y, b, DT)
                        else:
                            wait(e, n_sum, b, j - 1)
                        e.dma_start(side[j % 2][:, :], x[b, j * P:(j + 1) * P, :]).then_inc(n_side[j % 2].sem, 16)
                    q.put(OUT[j] + 1, 0, side_x)

                    def store(j=j):
                        wait(e, n_sum, b, j + 1)
                        e.dma_start(out[b, j * P:(j + 1) * P, :], ob[j % 2][:, :]).then_inc(n_store[j % 2].sem, 16)
                    q.put(OUT[j] + 2, 9, store)

            loads = [(ident[:, :], ident_in[0]), (ident_had, ident_in[1]),
                     (wx_sb[:, :, :].rearrange("p a b -> p (a b)"), w_x), (wdt_sb[0:RANK, :], w_dt), (a_sb[:, :], a_log),
                     (cw[:, :], conv_w), (ch[:, :, :].rearrange("p a b -> p (a b)"), chan), (bias_sb, bias)]
            assert len(loads) == LOADS
            for to, src in loads:
                e.dma_start(to, src).then_inc(p_load.sem, 16)
            q = Slots()
            norm(q, 0)
            q.at[NORM[-1]], late = q.at[NORM[-1]][:0], q.at[NORM[-1]]
            for s in range(LAST):
                q.run(s, [])
            for i in range(2):
                e.dma_start(acc[:, i * HALF:(i + 1) * HALF, :, :].rearrange("p d a b -> p (d a b)"),
                            w_out[:, i * HALF * DM:(i + 1) * HALF * DM]).then_inc(p_wout.sem, 16)
            for _, task in late:
                task()
            for r in range(5):
                e.dma_start(f_slot(r), factors[r].rearrange("p (a b) -> p a b", a=KT)).then_inc(p_f[r].sem, 16)
            q = Slots()
            front(q, 0)
            norm(q, 1)
            for s in range(LAST):
                q.run(s, [])
            for r in range(5, FACTORS):
                wait(e, p_fadd, 0, r - 4)
                e.dma_start(f_slot(r), factors[r].rearrange("p (a b) -> p a b", a=KT)).then_inc(p_f[r].sem, 16)
            b_load(0, 0)()

            def round_(t, has_front, has_norm, has_back):
                q = Slots()
                if has_front:
                    front(q, t + 1)
                if has_norm:
                    norm(q, t + 2)
                if has_back:
                    back(q, t - 1)
                for n in range(1, NS):
                    q.put(max(0, 2 * n - 2), 5, b_load(t, n))
                if has_front:
                    q.put(STEPS - 1, 9, b_load(t + 1, 0))
                for s in range(STEPS):
                    q.run(s, [])

            rounds(e, round_)
            q = Slots()
            back(q, BATCH - 1)
            for s in range(LAST):
                q.run(s, [])
            for i in range(2):
                wait(e, n_store[i], BATCH - 1, TT // 2)


def kernel(**inputs):
    from concourse import bacc
    from concourse.bass_utils import run_bass_kernel_spmd

    a = {k.removeprefix("L0_attn_"): np.asarray(v) for k, v in inputs.items()}

    def tiles(v, n):
        return np.ascontiguousarray(v.reshape(n, P, -1).transpose(1, 0, 2).reshape(P, -1))

    h = np.array([[1.0]])
    while h.shape[0] < P:
        h = np.block([[h, h], [h, -h]])
    had = (h / (4 * DI ** 0.5)).astype(np.float32)
    w_in = a["W_in"]
    arrays = {
        "x": a["hidden_states"],
        "w_in": np.ascontiguousarray(w_in.reshape(2 * DT, P, KT, P).transpose(0, 3, 2, 1).reshape(2 * DT, P, KT * P)),
        "w_x": tiles(a["W_x"].T, DT),
        "w_dt": np.ascontiguousarray(a["W_dt"].T),
        "w_out": tiles(a["W_out"].T, DT),
        "a_log": tiles(a["A_log"], DT),
        "conv_w": tiles(a["conv_w"], DT),
        "chan": np.concatenate([tiles(a[n].reshape(-1, 1), DT) for n in ("conv_b", "dt_bias", "D")], axis=1),
        "factors": np.ascontiguousarray(a["L0_ffn_factors"].reshape(FACTORS, KT, P, DM).transpose(0, 2, 1, 3)
                                        .reshape(FACTORS, P, KT * DM)),
        "bias": a["L0_ffn_bias"].reshape(1, DM),
        "consts": np.stack([np.eye(P, dtype=np.float32), had]),
    }
    nc = bacc.Bacc("TRN2", target_bir_lowering=False, num_devices=1)
    ap = {n: nc.dram_tensor(f"in_{n}", v.shape, F32, kind="ExternalInput").ap() for n, v in arrays.items()}
    u_dram = nc.dram_tensor("u_dram", [BATCH, DT, P, TOK], F32, kind="Internal").ap()
    xn_dram = nc.dram_tensor("xn_dram", [BATCH, P, KT * TOK], F32, kind="Internal").ap()
    b_dram = nc.dram_tensor("b_dram", [BATCH, NS, TOK], F32, kind="Internal").ap()
    out = nc.dram_tensor("out", [BATCH, TOK, DM], F32, kind="ExternalOutput").ap()
    program(nc, ap["x"], ap["w_in"], ap["w_x"], ap["w_dt"], ap["w_out"], ap["a_log"], ap["conv_w"], ap["chan"],
            ap["factors"], ap["bias"], None, ap["consts"], u_dram, xn_dram, b_dram, out)
    r = run_bass_kernel_spmd(nc, [{f"in_{n}": v for n, v in arrays.items()}], core_ids=[0])
    return r.results[0]["out"]
```

```python
from contextlib import ExitStack

import numpy as np

import concourse.bass as bass
from concourse import mybir

F32 = mybir.dt.float32
ALU = mybir.AluOpType
ACT = mybir.ActivationFunctionType

APART = (mybir.EngineType.Activation, mybir.EngineType.Pool, mybir.EngineType.SP)
P = 128
BATCH, TOK, DM = 16, 512, 512
DI = 2 * DM
NS = 16
TAPS = 4
RANK = DM // 16
FACTORS = 8
KT = DM // P
DT = DI // P
TT = TOK // P
HALF = DT // 2
STEPS = 2 * NS
SCANS = HALF * STEPS
MACS = TT * STEPS
NX = RANK + 2 * NS
EPS = 1e-5

X_TILE = [1 + 2 * i for i in range(DT)]
X_PROJ = 17
DT_TILE = [20 + i for i in range(DT)]
NORM = [28 + j for j in range(TT)]
Z_TILE = [2 * i for i in range(DT)]
FFN = [16, 17, 18, 20]
OUT = [21 + 2 * j for j in range(TT)]
AT = {
    "x_tile": (.5, .5, 1, 1),
    "tap": (2.25, 1.625, 1.875, 2),
    "x_tanh": 3.25,
    "x_silu": 2.625,
    "x_proj": (.5, .5, 1, 1, 1.5, 1.5, 2, 2),
    "take_xdbl": 3.25,
    "c_turn": 3,
    "take_c": 3.5,
    "dt_tile": 1,
    "relu": 2,
    "sp_exp": 2.5,
    "sp_ln": 2.75,
    "sp_add": 2.5,
    "dtu": 3,
    "stats": (-2, -1.75, -1.5),
    "rstd": -0.5,
    "shift": -.625,
    "normalise": .5,
    "n_turn": 1,
    "xnt": 2,
    "z_tile": (.5, .5, 1, 1),
    "z_tanh": 2,
    "z_silu": 1.375,
    "y_turn": 2,
    "skip": 2.125,
    "gate": 3,
    "ffn": (.5, .5, 1, 1),
    "f_tanh": 2,
    "f_silu": 1.375,
    "out": (.5, .5, 1, 1, 1.5, 1.5, 2, 2),
    "out_gate": 2.25,
    "residual": 3.5,
}
LN_TABLE, TANH_TABLE = 22.25, 30.25
LAST = 36


class Count:

    def __init__(self, sem, per, unit, waited):
        self.sem, self.per, self.unit, self.waited = sem, per, unit, waited

    def upto(self, batch, n):
        if isinstance(batch, int):
            return (batch * self.per + n) * self.unit
        return batch * (self.per * self.unit) + n * self.unit


def wait(e, count, batch, n, apart=False):
    value = count.upto(batch, n)
    if not isinstance(value, int) or value > 0:
        e.wait_ge(count.sem, value)
        if not isinstance(value, int) and (apart or e.engine in APART):
            e.sem_inc(count.waited, 1)


class Slots:

    def __init__(self, end=None):
        self.at, self.end, self.late = {}, end, False

    def put(self, time, task):
        if self.end is not None:
            if (time >= self.end) != self.late:
                return
            time -= self.end * self.late
        step = int(time)
        self.at.setdefault(step, []).append((time - step, task))

    def run(self, step, own):
        extra = sorted(self.at.get(step, []), key=lambda x: x[0])
        for i, instruction in enumerate(own):
            while extra and extra[0][0] * len(own) <= i:
                extra.pop(0)[1]()
            instruction()
        for _, task in extra:
            task()


def program(nc, x, w_in, w_x, w_dt, w_out, a_log, conv_w, chan, factors, bias, had, ident_in,
            u_dram, xn_dram, b_dram, out):
    ctx = ExitStack()
    with ctx:
        def sb(name, shape):
            return ctx.enter_context(nc.sbuf_tensor(name, shape, F32))

        def ps(name, shape):
            return ctx.enter_context(nc.psum_tensor(name, shape, F32))

        waited = ctx.enter_context(nc.semaphore("waited"))

        def count(name, per, unit=1):
            return Count(ctx.enter_context(nc.semaphore(name)), per, unit, waited)

        wx_sb = sb("wx_sb", [P, DT, NX])
        wdt_sb = sb("wdt_sb", [RANK + 1, DI])
        wc_sb = sb("wc_sb", [P, DT, DM])
        f_sb = sb("f_sb", [P, KT, DM])
        ident = sb("ident", [P, P])
        a_sb = sb("a_sb", [P, DT * NS])
        cw = sb("cw", [P, DT * TAPS])
        ch = sb("ch", [P, 3, DT])
        bias_sb = wdt_sb[RANK:RANK + 1, 0:DM]
        ones = wdt_sb[RANK:RANK + 1, DM:DM + P]
        w_xt = [sb(f"w_xt{i}", [P, KT, P]) for i in range(2)]
        w_zt = [sb(f"w_zt{i}", [P, KT, P]) for i in range(2)]
        delta = sb("delta", [P, 2, DT, TOK])
        dtu = sb("dtu", [P, 2, DT, TOK])
        acc = sb("acc", [P, DT, TT, P])
        acc_f = sb("acc_f", [P, DT, TT, P])
        h = [sb(f"h{i}", [P, HALF, TOK]) for i in range(2)]
        dbu = [sb(f"dbu{i}", [P, 2, TOK]) for i in range(2)]
        b_rep = [sb(f"b_rep{i}", [P, TOK]) for i in range(2)]
        c_now = sb("c_now", [P, TT, NS])
        c_next = sb("c_next", [P, TT, NS])
        xnt = sb("xnt", [P, KT, TOK])
        xnt_b = sb("xnt_b", [P, KT, TOK])
        x_in = [buf[:, :, :].rearrange("p a b -> p (a b)") for buf in w_xt + w_zt]
        stats = sb("stats", [P, 2, 6])
        mv = sb("mv", [P, 2, 2])
        rs = sb("rs", [P, 2, 2])
        power = sb("power", [P, 1])
        side = [sb(f"side{i}", [P, TOK]) for i in range(2)]
        sp = [sb(f"sp{i}", [P, TOK]) for i in range(2)]
        sz = sb("sz", [P, TOK])
        yb = sb("yb", [P, TOK])
        ob = [sz, yb]
        ident_had = sz[:, 0:P]
        gf = sb("gf", [P, TT, DM])
        xdbl = sb("xdbl", [NX, TOK])

        decay = [ps(f"decay{i}", [P, TOK]) for i in range(3)]
        ht = [ps(f"ht{i}", [P, HALF, P]) for i in range(2)]
        pf = ps("pf", [P, TOK])
        pb = ps("pb", [P, TOK])
        px = ps("px", [P, TOK])
        back_bank = [pb, px]

        n_decay = count("n_decay", SCANS)
        n_dbu = count("n_dbu", SCANS // 2)
        n_scan = count("n_scan", SCANS)
        n_ht = count("n_ht", MACS)
        n_mac = count("n_mac", MACS)
        n_brep = [count(f"n_brep{i}", NS // 2, 16) for i in range(2)]
        n_xin = [count(f"n_xin{j}", 1, 16) for j in range(TT)]
        n_stat = count("n_stat", 3 * TT)
        n_shift = count("n_shift", TT)
        n_rstd = count("n_rstd", TT)
        n_norm = count("n_norm", TT)
        n_xturn = count("n_xturn", TT)
        n_xnt = count("n_xnt", TT)
        n_xspill = count("n_xspill", 1, 16)
        n_wx = [count(f"n_wx{i}", DT // 2, 16) for i in range(2)]
        n_in = count("n_in", DT)
        n_tap0 = count("n_tap0", DT)
        n_tap = count("n_tap", DT * (TAPS - 1))
        n_tanh = count("n_tanh", DT)
        n_u = count("n_u", DT)
        n_uspill = count("n_uspill", DT, 16)
        n_xproj = count("n_xproj", 1)
        n_xdbl = count("n_xdbl", 1)
        n_bspill = count("n_bspill", 1, 16)
        n_cturn = count("n_cturn", 1)
        n_cnext = count("n_cnext", 1)
        n_cnow = count("n_cnow", 1)
        n_dt = count("n_dt", DT)
        n_relu = count("n_relu", DT)
        n_abs = count("n_abs", DT)
        n_exp = count("n_exp", DT)
        n_ln = count("n_ln", DT)
        n_delta = count("n_delta", DT)
        n_dtu = count("n_dtu", DT)
        n_xback = count("n_xback", 1, 16)
        n_wz = [count(f"n_wz{i}", DT // 2, 16) for i in range(2)]
        n_z = count("n_z", DT)
        n_ztanh = count("n_ztanh", DT)
        n_sz = count("n_sz", DT)
        n_side = [count(f"n_side{i}", (DT + TT) // 2, 16) for i in range(2)]
        n_yturn = count("n_yturn", DT)
        n_y = count("n_y", DT)
        n_g = count("n_g", DT)
        n_ffn = count("n_ffn", TT)
        n_ftanh = count("n_ftanh", TT)
        n_gf = count("n_gf", TT)
        n_out = count("n_out", TT)
        n_o = count("n_o", TT)
        n_sum = count("n_sum", TT)
        n_store = [count(f"n_store{i}", TT // 2, 16) for i in range(2)]
        p_load = count("p_load", 1, 16)
        p_wout = count("p_wout", 1, 16)
        p_f = [count(f"p_f{i}", 1, 16) for i in range(FACTORS)]
        p_fadd = count("p_fadd", 1)
        p_fscale = count("p_fscale", 1)
        p_act = count("p_act", 1)
        p_dve = count("p_dve", 1)
        p_h = count("p_h", 1)
        p_hcopy = count("p_hcopy", 1)
        p_fold = count("p_fold", 1)

        LOADS = 8
        f_part = [f_sb] + [buf[:, 1, i * KT:(i + 1) * KT, :] for buf in (delta, dtu) for i in range(2)]

        def f_slot(r):
            return f_sb[:, :, :] if r == 0 else f_part[1 + (r - 1) % 4]

        def turn(b):
            return b % 2

        block = ctx.enter_context(nc.Block())

        def fill(t, has_front, has_norm, has_back, front, norm, back):
            q = Slots(STEPS if not isinstance(t, int) or t < BATCH else LAST)
            if has_front:
                front(q, t + 1)
            if has_norm:
                norm(q, t + 2)
            if has_back:
                back(q, t - 1)
            q.late, q.end = True, STEPS
            if not isinstance(t, int) or 0 < t < BATCH:
                front(q, t)
            if not isinstance(t, int) or 0 < t < BATCH - 1:
                norm(q, t + 1)
            if not isinstance(t, int) or t > 1:
                back(q, t - 2)
            q.late = False
            return q

        def rounds(e, round_):
            round_(0, True, True, False)
            round_(1, True, True, True)
            with e.Fori(2, BATCH - 2) as t:
                round_(t, True, True, True)
            round_(BATCH - 2, True, False, True)
            round_(BATCH - 1, False, False, True)

        @block.tensor
        def _(e):
            def turns(b, s, j):
                def task():
                    wait(e, n_scan, b, HALF * (s + 1))
                    wait(e, n_mac, b, TT * s + j - 1)
                    for i in range(HALF):
                        mm = e.transpose(ht[j % 2][:, i, :], h[s % 2][:, i, j * P:(j + 1) * P], ident[:, :])
                    mm.then_inc(n_ht.sem, 1)
                return task

            def norm(q, b):
                for j in range(TT):
                    def task(j=j):
                        wait(e, n_norm, b, j + 1)
                        if j == 0:
                            wait(e, n_abs, b, 0)
                        else:
                            wait(e, n_xnt, b, j)
                        for k in range(KT):
                            mm = e.transpose(pf[:, k * P:(k + 1) * P], x_in[j][:, k * P:(k + 1) * P], ident[:, :])
                        mm.then_inc(n_xturn.sem, 1)
                    q.put(NORM[j] + AT["n_turn"], task)

            def front(q, b):
                for i in range(DT):
                    def x_tile(k, i=i):
                        if k == 0:
                            wait(e, n_xnt, b, TT)
                            wait(e, n_tap, b, (TAPS - 1) * i)
                            wait(e, n_wx[i % 2], b, i // 2 + 1)
                        mm = e.matmul(pf[:, :], w_xt[i % 2][:, k, :], xnt[:, k, :], start=k == 0, stop=k == KT - 1)
                        if k == KT - 1:
                            mm.then_inc(n_in.sem, 1)
                    for k in range(KT):
                        q.put(X_TILE[i] + AT["x_tile"][k], lambda k=k, f=x_tile: f(k))

                def x_proj(i):
                    if i == 0:
                        wait(e, n_tap, b, (TAPS - 1) * DT)
                    wait(e, n_u, b, i + 1)
                    mm = e.matmul(pf[0:NX, :], wx_sb[:, i, :], dtu[:, turn(b), i, :], start=i == 0, stop=i == DT - 1)
                    if i == DT - 1:
                        mm.then_inc(n_xproj.sem, 1)
                for i in range(DT):
                    q.put(X_PROJ + AT["x_proj"][i], lambda i=i: x_proj(i))

                def c_turn():
                    wait(e, n_xdbl, b, 1, apart=True)
                    for j in range(TT):
                        mm = e.transpose(pf[:, j * NX:(j + 1) * NX], xdbl[:, j * P:(j + 1) * P], ident[0:NX, 0:NX])
                    mm.then_inc(n_cturn.sem, 1)
                q.put(X_PROJ + AT["c_turn"], c_turn)

                for i in range(DT):
                    def dt_tile(i=i):
                        if i == 0:
                            wait(e, n_cnext, b, 1)
                        else:
                            wait(e, n_abs, b, i)
                            wait(e, n_relu, b, i)
                        e.matmul(pf[:, :], wdt_sb[0:RANK, i * P:(i + 1) * P], xdbl[0:RANK, :],
                                 start=True, stop=True).then_inc(n_dt.sem, 1)
                    q.put(DT_TILE[i] + AT["dt_tile"], dt_tile)

            def back(q, b):
                for i in range(DT):
                    def z_tile(k, i=i):
                        if k == 0:
                            wait(e, n_xback, b, 1)
                            if i == 0:
                                wait(e, n_o, b, 0)
                            else:
                                wait(e, n_y, b, i)
                            wait(e, n_wz[i % 2], b, i // 2 + 1)
                        mm = e.matmul(pb[:, :], w_zt[i % 2][:, k, :], xnt_b[:, k, :], start=k == 0, stop=k == KT - 1)
                        if k == KT - 1:
                            mm.then_inc(n_z.sem, 1)
                    for k in range(KT):
                        q.put(Z_TILE[i] + AT["z_tile"][k], lambda k=k, f=z_tile: f(k))

                    def y_turn(i=i):
                        wait(e, n_mac, b, MACS)
                        wait(e, n_sz, b, i + 1)
                        for j in range(TT):
                            mm = e.transpose(pb[:, j * P:(j + 1) * P], acc_f[:, i, j, :], ident[:, :])
                        mm.then_inc(n_yturn.sem, 1)
                    q.put(Z_TILE[i] + AT["y_turn"], y_turn)

                for j in range(TT):
                    def ffn(k, j=j):
                        if k == 0:
                            if j == 0:
                                wait(e, n_y, b, DT)
                            elif j == 1:
                                wait(e, n_u, b + 3 if not isinstance(b, int) else min(b + 3, BATCH), 0)
                            else:
                                wait(e, n_gf, b, j - 1)
                        e.matmul(back_bank[j % 2][:, :], xnt_b[:, k, j * P:(j + 1) * P], f_sb[:, k, :], start=k == 0, stop=False)
                        if k == KT - 1:
                            e.matmul(back_bank[j % 2][:, :], ones, bias_sb, start=False, stop=True).then_inc(n_ffn.sem, 1)
                    for k in range(KT):
                        q.put(FFN[j] + AT["ffn"][k], lambda k=k, f=ffn: f(k))

                    def out_tile(i, j=j):
                        if i == 0:
                            wait(e, n_g, b, DT)
                            if j < 2:
                                wait(e, n_gf, b, TT - 1 + j)
                            else:
                                wait(e, n_o, b, j - 1)
                        g = acc_f[:, i, :, :].rearrange("p a b -> p (a b)")
                        mm = e.matmul(back_bank[j % 2][:, :], g[:, j * P:(j + 1) * P], wc_sb[:, i, :], start=i == 0, stop=i == DT - 1)
                        if i == DT - 1:
                            mm.then_inc(n_out.sem, 1)
                    for i in range(DT):
                        q.put(OUT[j] + AT["out"][i], lambda i=i, f=out_tile: f(i))

            wait(e, p_load, 0, LOADS)
            q = Slots()
            norm(q, 0)
            for s in range(LAST):
                q.run(s, [])
            wait(e, p_wout, 0, 2)
            for i in range(DT):
                bank = (decay + [pb])[i % 4][:, :]
                if i >= 4:
                    wait(e, p_hcopy, 0, i - 3)
                e.matmul(bank, ident_had, acc[:, i, :, :].rearrange("p a b -> p (a b)"),
                         start=True, stop=True).then_inc(p_h.sem, 1)
            q = Slots()
            front(q, 0)
            norm(q, 1)
            for s in range(LAST):
                q.run(s, [])

            def round_(t, has_front, has_norm, has_back):
                q = fill(t, has_front, has_norm, has_back, front, norm, back)
                for s in range(STEPS):
                    if s == 0:
                        own = [turns(t - 1, STEPS - 1, j) for j in range(TT)] if has_back else []
                    else:
                        own = [turns(t, s - 1, j) for j in range(TT)]
                    q.run(s, own)

            wait(e, p_fold, 0, 24)
            wait(e, p_fscale, 0, 1)
            rounds(e, round_)
            for j in range(TT):
                turns(BATCH - 1, STEPS - 1, j)()
            q = fill(BATCH, False, False, True, None, None, back)
            for s in range(LAST):
                q.run(s, [])

        @block.scalar
        def _(e):
            def decays(b, s, i):
                q, tile = HALF * s + i, HALF * (s % 2) + i

                def task():
                    if s == 0 and i == 0:
                        wait(e, n_delta, b, DT)
                    wait(e, n_scan, b, q - 2 if q >= 2 else q - 1)
                    n = tile * NS + s // 2
                    e.activation(decay[q % 3][:, :], delta[:, turn(b), tile, :], ACT.Exp,
                                 bias=0.0, scale=a_sb[:, n:n + 1]).then_inc(n_decay.sem, 1)
                return task

            def norm(q, b):
                for j in range(TT):
                    def normalise(j=j):
                        wait(e, n_shift, b, j + 1)
                        e.activation(x_in[j], x_in[j], ACT.Identity, bias=rs[:, j % 2, 1:2],
                                     scale=rs[:, j % 2, 0:1]).then_inc(n_norm.sem, 1)
                    q.put(NORM[j] + AT["normalise"], normalise)

                    def evacuate(j=j):
                        wait(e, n_xturn, b, j + 1)
                        if j == 0:
                            wait(e, n_in, b, 0)
                            wait(e, n_xspill, b, 0)
                        e.copy(xnt[:, :, j * P:(j + 1) * P],
                               pf[:, :].rearrange("p (k b) -> p k b", k=KT)).then_inc(n_xnt.sem, 1)
                    q.put(NORM[j] + AT["xnt"], evacuate)

            def front(q, b):
                for i in range(DT):
                    def tap0(i=i):
                        if i == 0:
                            wait(e, n_dbu, b - 1, 0) if not isinstance(b, int) or b >= 1 else None
                        wait(e, n_in, b, i + 1)
                        k = i * TAPS + TAPS - 1
                        e.activation(dtu[:, turn(b), i, :], pf[:, :], ACT.Identity, bias=ch[:, 0, i:i + 1],
                                     scale=cw[:, k:k + 1]).then_inc(n_tap0.sem, 1)
                    q.put(X_TILE[i] + AT["tap"][0], tap0)

                    def tanh(i=i):
                        wait(e, n_tap, b, (TAPS - 1) * (i + 1))
                        wait(e, n_u, b, i)
                        if i == 0 and not (isinstance(b, int) and b < 3):
                            wait(e, n_o, b - 2, 0)
                        e.activation(px[:, :], dtu[:, turn(b), i, :], ACT.Tanh).then_inc(n_tanh.sem, 1)
                    q.put(X_TILE[i] + AT["x_tanh"], tanh)

                def take_xdbl():
                    wait(e, n_xproj, b, 1)
                    wait(e, n_dt, b, 0)
                    wait(e, n_bspill, b, 0)
                    e.copy(xdbl[:, :], pf[0:NX, :]).then_inc(n_xdbl.sem, 1)
                q.put(X_PROJ + AT["take_xdbl"], take_xdbl)

                for i in range(DT):
                    def relu(i=i):
                        wait(e, n_dt, b, i + 1)
                        e.activation(delta[:, turn(b), i, :], pf[:, :], ACT.Relu, bias=ch[:, 1, i:i + 1],
                                     scale=1.0).then_inc(n_relu.sem, 1)
                        if i >= 2:
                            wait(e, n_delta, b, i - 1)
                        elif i == 1 and not (isinstance(b, int) and b < 2):
                            wait(e, n_sz, b - 1, 0)
                        e.activation(sp[(i + 1) % 2][:, :], pf[:, :], ACT.Abs, bias=ch[:, 1, i:i + 1],
                                     scale=1.0).then_inc(n_abs.sem, 1)
                    q.put(DT_TILE[i] + AT["relu"], relu)

                    def exp(i=i):
                        wait(e, n_abs, b, i + 1)
                        e.activation(sp[(i + 1) % 2][:, :], sp[(i + 1) % 2][:, :], ACT.Exp, scale=-1.0).then_inc(n_exp.sem, 1)
                    q.put(DT_TILE[i] + AT["sp_exp"], exp)

                    def ln(i=i):
                        wait(e, n_exp, b, i + 1)
                        e.activation(sp[(i + 1) % 2][:, :], sp[(i + 1) % 2][:, :], ACT.Ln, bias=1.0).then_inc(n_ln.sem, 1)
                    q.put(DT_TILE[i] + AT["sp_ln"], ln)
                q.put(LN_TABLE, lambda: e.preload_act_table_set("natural_log_exp_and_others"))
                q.put(TANH_TABLE, lambda: e.preload_act_table_set("exp_and_others"))

            def back(q, b):
                for i in range(DT):
                    def z_tanh(i=i):
                        if i == 0:
                            wait(e, n_delta, b + 1, DT) if not isinstance(b, int) or b < BATCH - 1 else None
                        wait(e, n_z, b, i + 1)
                        e.activation(sp[0][:, :], pb[:, :], ACT.Tanh, scale=0.5).then_inc(n_ztanh.sem, 1)
                    q.put(Z_TILE[i] + AT["z_tanh"], z_tanh)
                for j in range(TT):
                    def f_tanh(j=j):
                        wait(e, n_ffn, b, j + 1)
                        if j < 2:
                            wait(e, n_g, b, DT)
                        else:
                            wait(e, n_gf, b, j - 1)
                        e.activation(ob[j % 2][:, :], back_bank[j % 2][:, :], ACT.Tanh, scale=0.5).then_inc(n_ftanh.sem, 1)
                    q.put(FFN[j] + AT["f_tanh"], f_tanh)

            wait(e, p_load, 0, LOADS)
            e.activation(a_sb[:, :], a_sb[:, :], ACT.Exp).then_inc(p_act.sem, 1)
            e.mul(cw[:, :], cw[:, :], 0.5).then_inc(p_act.sem, 1)
            e.mul(ch[:, 0, :], ch[:, 0, :], 0.5).then_inc(p_act.sem, 1)
            wait(e, p_act, 0, 1)
            e.mul(a_sb[:, :], a_sb[:, :], -1.0).then_inc(p_act.sem, 1)
            wait(e, p_act, 0, 4)
            q = Slots()
            norm(q, 0)
            for s in range(LAST):
                q.run(s, [])
            for i in range(DT):
                bank = (decay + [pb])[i % 4][:, :]
                wait(e, p_h, 0, i + 1)
                e.copy(acc_f[:, i, :, :], bank.rearrange("p (a b) -> p a b", a=TT)).then_inc(p_hcopy.sem, 1)
            q = Slots()
            front(q, 0)
            norm(q, 1)
            for s in range(LAST):
                q.run(s, [])
            wait(e, p_fadd, 0, FACTORS - 1)
            e.mul(f_sb[:, :, :], f_sb[:, :, :], FACTORS ** -0.5).then_inc(p_fscale.sem, 1)

            def round_(t, has_front, has_norm, has_back):
                q = fill(t, has_front, has_norm, has_back, front, norm, back)
                for s in range(STEPS):
                    q.run(s, [decays(t, s, i) for i in range(HALF)])

            rounds(e, round_)
            q = fill(BATCH, False, False, True, None, None, back)
            for s in range(LAST):
                q.run(s, [])

        @block.gpsimd
        def _(e):
            def inputs(b, s, p):
                q, tile = 2 * s + p, HALF * (s % 2) + 2 * p
                n = s // 2

                def task():
                    if s == 0 and p == 0:
                        wait(e, n_dtu, b, DT)
                    wait(e, n_brep[n % 2], b, n // 2 + 1)
                    wait(e, n_scan, b, 2 * (q - 1))
                    e.tensor_tensor(dbu[q % 2][:, :, :], dtu[:, turn(b), tile:tile + 2, :],
                                    b_rep[n % 2][:, None, :].broadcast_to([P, 2, TOK]), ALU.mult).then_inc(n_dbu.sem, 1)
                return task

            def front(q, b):
                for i in range(DT):
                    def add(i=i):
                        wait(e, n_ln, b, i + 1)
                        e.tensor_tensor(delta[:, turn(b), i, :], delta[:, turn(b), i, :], sp[(i + 1) % 2][:, :],
                                        ALU.add).then_inc(n_delta.sem, 1)
                    q.put(DT_TILE[i] + AT["sp_add"], add)

                    def mult(i=i):
                        wait(e, n_delta, b, i + 1)
                        if i == 0:
                            wait(e, n_uspill, b, DT)
                            wait(e, n_xproj, b, 1)
                        e.tensor_tensor(dtu[:, turn(b), i, :], dtu[:, turn(b), i, :], delta[:, turn(b), i, :],
                                        ALU.mult).then_inc(n_dtu.sem, 1)
                    q.put(DT_TILE[i] + AT["dtu"], mult)

            def back(q, b):
                for i in range(DT):
                    def gate(i=i):
                        wait(e, n_y, b, i + 1)
                        wait(e, n_sz, b, i + 1)
                        e.tensor_tensor(acc_f[:, i, :, :].rearrange("p a b -> p (a b)"), yb[:, :], sz[:, :],
                                        ALU.mult).then_inc(n_g.sem, 1)
                    q.put(Z_TILE[i] + AT["gate"], gate)
                for j in range(TT):
                    def residual(j=j):
                        wait(e, n_o, b, j + 1)
                        wait(e, n_side[j % 2], b, (DT + j) // 2 + 1)
                        e.tensor_tensor(ob[j % 2][:, :], ob[j % 2][:, :], side[j % 2][:, :],
                                        ALU.add).then_inc(n_sum.sem, 1)
                    q.put(OUT[j] + AT["residual"], residual)

            def norm(q, b):
                for j in range(TT):
                    def rstd(j=j, r=j % 2):
                        wait(e, n_stat, b, 3 * j + 3)
                        if j >= 2:
                            wait(e, n_norm, b, j - 1)
                        else:
                            wait(e, n_norm, b, 0)
                        e.tensor_tensor(rs[:, r, 0:1], mv[:, r, 1:2], power[:, :], ALU.pow).then_inc(n_rstd.sem, 1)
                    q.put(NORM[j] + AT["rstd"], rstd)

            wait(e, p_dve, 0, 1)
            q = Slots()
            norm(q, 0)
            for s in range(LAST):
                q.run(s, [])
            def add_factors(rs_):
                for r in rs_:
                    wait(e, p_f[0], 0, 1)
                    wait(e, p_f[r], 0, 1)
                    wait(e, p_fadd, 0, r - 1)
                    e.tensor_tensor(f_sb[:, :, :], f_sb[:, :, :], f_slot(r), ALU.add).then_inc(p_fadd.sem, 1)

            add_factors(range(1, 5))
            q = Slots()
            front(q, 0)
            norm(q, 1)
            for s in range(LAST):
                q.run(s, [])
            add_factors(range(5, FACTORS))

            def round_(t, has_front, has_norm, has_back):
                q = fill(t, has_front, has_norm, has_back, front, norm, back)
                for s in range(STEPS):
                    q.run(s, [inputs(t, s, p) for p in range(2)])

            rounds(e, round_)
            q = fill(BATCH, False, False, True, None, None, back)
            for s in range(LAST):
                q.run(s, [])

        @block.vector
        def _(e):
            def scan(b, s, i):
                q = HALF * s + i

                def task():
                    wait(e, n_decay, b, q + 1)
                    if i % 2 == 0:
                        wait(e, n_dbu, b, q // 2 + 1)
                    e.tensor_tensor_scan(h[s % 2][:, i, :], decay[q % 3][:, :], dbu[q // 2 % 2][:, i % 2, :],
                                         0.0, ALU.mult, ALU.add).then_inc(n_scan.sem, 1)
                return task

            def mac(b, s, j):
                n, half = s // 2, s % 2

                def task():
                    tiles = slice(half * HALF, (half + 1) * HALF)
                    wait(e, n_ht, b, TT * s + j + 1)
                    if s == 0 and j == 0:
                        wait(e, n_cnow, b, 1)
                    c = c_now[:, j, n:n + 1]
                    if n == 0:
                        op = e.tensor_scalar(acc[:, tiles, j, :], ht[j % 2][:, :, :], c, None, ALU.mult)
                    else:
                        wait(e, n_mac, b, TT * (s - 2) + j + 1)
                        if n == NS - 1 and half == 0 and j == 0:
                            wait(e, n_out, b, 0)
                        to = acc_f if n == NS - 1 else acc
                        op = e.scalar_tensor_tensor(out=to[:, tiles, j, :], in0=ht[j % 2][:, :, :], scalar=c,
                                                    in1=acc[:, tiles, j, :], op0=ALU.mult, op1=ALU.add)
                    op.then_inc(n_mac.sem, 1)
                return task

            def norm(q, b):
                for j in range(TT):
                    r = j % 2

                    def bn(j=j, r=r):
                        wait(e, n_xin[j], b, 1)
                        e.bn_stats(stats[:, r, :], x_in[j]).then_inc(n_stat.sem, 1)

                    def aggr(j=j, r=r):
                        wait(e, n_stat, b, 3 * j + 1, apart=True)
                        e.bn_aggr(mv[:, r, :], stats[:, r, :]).then_inc(n_stat.sem, 1)

                    def eps(j=j, r=r):
                        wait(e, n_stat, b, 3 * j + 2)
                        if j >= 2:
                            wait(e, n_norm, b, j - 1)
                        else:
                            wait(e, n_norm, b, 0)
                        e.tensor_scalar(mv[:, r, 1:2], mv[:, r, 1:2], EPS, None, ALU.add).then_inc(n_stat.sem, 1)

                    def shift(j=j, r=r):
                        wait(e, n_rstd, b, j + 1)
                        e.tensor_scalar(rs[:, r, 1:2], mv[:, r, 0:1], rs[:, r, 0:1], -1.0, ALU.mult,
                                        ALU.mult).then_inc(n_shift.sem, 1)
                    for k, f in enumerate((bn, aggr, eps)):
                        q.put(NORM[j] + AT["stats"][k], f)
                    q.put(NORM[j] + AT["shift"], shift)

            def front(q, b):
                for i in range(DT):
                    for k in range(1, TAPS):
                        def tap(i=i, k=k):
                            w = cw[:, i * TAPS + TAPS - 1 - k:i * TAPS + TAPS - k]
                            v = dtu[:, turn(b), i, k:TOK]
                            wait(e, n_tap0, b, i + 1)
                            wait(e, n_tap, b, (TAPS - 1) * i + k - 1)
                            e.scalar_tensor_tensor(out=v, in0=pf[:, 0:TOK - k], scalar=w, in1=v, op0=ALU.mult,
                                                   op1=ALU.add).then_inc(n_tap.sem, 1)
                        q.put(X_TILE[i] + AT["tap"][k], tap)

                    def silu(i=i):
                        wait(e, n_tanh, b, i + 1)
                        e.scalar_tensor_tensor(out=dtu[:, turn(b), i, :], in0=px[:, :], scalar=1.0,
                                               in1=dtu[:, turn(b), i, :], op0=ALU.add, op1=ALU.mult).then_inc(n_u.sem, 1)
                    q.put(X_TILE[i] + AT["x_silu"], silu)

                def take_c():
                    wait(e, n_cturn, b, 1)
                    wait(e, n_cnow, b, 0)
                    e.tensor_copy(c_next[:, :, :], pf[:, 0:TT * NX].rearrange("p (j x) -> p j x", j=TT)
                                  [:, :, RANK + NS:NX]).then_inc(n_cnext.sem, 1)
                q.put(X_PROJ + AT["take_c"], take_c)

            def take_over(b):
                def task():
                    wait(e, n_cnext, b, 1)
                    wait(e, n_mac, b, 0)
                    e.tensor_copy(c_now[:, :, :], c_next[:, :, :]).then_inc(n_cnow.sem, 1)
                return task

            def back(q, b):
                for i in range(DT):
                    def silu_z(i=i):
                        wait(e, n_ztanh, b, i + 1)
                        wait(e, n_g, b, i)
                        if i == 0:
                            wait(e, n_store[0], b, 0)
                        e.scalar_tensor_tensor(out=sz[:, :], in0=sp[0][:, :], scalar=1.0, in1=pb[:, :], op0=ALU.add,
                                               op1=ALU.mult).then_inc(n_sz.sem, 1)
                    q.put(Z_TILE[i] + AT["z_silu"], silu_z)

                    def skip(i=i):
                        wait(e, n_yturn, b, i + 1)
                        wait(e, n_side[i % 2], b, i // 2 + 1)
                        wait(e, n_g, b, i)
                        if i == 0:
                            wait(e, n_store[1], b, 0)
                        e.scalar_tensor_tensor(out=yb[:, :], in0=side[i % 2][:, :], scalar=ch[:, 2, i:i + 1],
                                               in1=pb[:, :], op0=ALU.mult, op1=ALU.add).then_inc(n_y.sem, 1)
                    q.put(Z_TILE[i] + AT["skip"], skip)
                for j in range(TT):
                    def silu_f(j=j):
                        wait(e, n_ftanh, b, j + 1)
                        e.scalar_tensor_tensor(out=gf[:, j, :], in0=ob[j % 2][:, :], scalar=1.0,
                                               in1=back_bank[j % 2][:, :], op0=ALU.add, op1=ALU.mult).then_inc(n_gf.sem, 1)
                    q.put(FFN[j] + AT["f_silu"], silu_f)

                    def gate(j=j):
                        wait(e, n_out, b, j + 1)
                        if j >= 2:
                            wait(e, n_store[j % 2], b, j // 2)
                        else:
                            wait(e, n_g, b, DT)
                        wait(e, n_gf, b, j + 1)
                        e.tensor_tensor(ob[j % 2][:, :], back_bank[j % 2][:, :], gf[:, j, :], ALU.mult).then_inc(n_o.sem, 1)
                    q.put(OUT[j] + AT["out_gate"], gate)

            e.memset(ones, 1.0)
            e.memset(power[:, :], -0.5).then_inc(p_dve.sem, 1)
            q = Slots()
            norm(q, 0)
            for s in range(LAST):
                q.run(s, [])
            q = Slots()
            front(q, 0)
            norm(q, 1)
            for s in range(LAST):
                q.run(s, [])
            flat = [t[:, :, :, :].rearrange("p d a b -> p d (a b)") for t in (acc_f, acc)]
            stage_from, stage_to = (flat[0], flat[1], flat[0]), (flat[1], flat[0], wc_sb)
            wait(e, p_hcopy, 0, DT)
            wait(e, p_h, 0, DT)
            for k in range(3):
                src, dst, d = stage_from[k], stage_to[k], 1 << k
                if k:
                    wait(e, p_fold, 0, DT * k)
                for i in range(DT):
                    lo, hi = i & ~d, i | d
                    e.tensor_tensor(dst[:, i, :], src[:, lo, :], src[:, hi, :],
                                    ALU.subtract if i & d else ALU.add).then_inc(p_fold.sem, 1)

            def round_(t, has_front, has_norm, has_back):
                q = fill(t, has_front, has_norm, has_back, front, norm, back)
                for s in range(STEPS):
                    if s == 0:
                        macs = [mac(t - 1, STEPS - 1, j) for j in range(TT)] if has_back else []
                    else:
                        macs = [mac(t, s - 1, j) for j in range(TT)]
                    own = [scan(t, s, i) for i in range(HALF)]
                    own = [task for pair in zip(own, macs) for task in pair] if macs else own
                    if s == 1:
                        own = [take_over(t)] + own
                    q.run(s, own)

            rounds(e, round_)
            for j in range(TT):
                mac(BATCH - 1, STEPS - 1, j)()
            q = fill(BATCH, False, False, True, None, None, back)
            for s in range(LAST):
                q.run(s, [])

        @block.sync
        def _(e):
            def b_load(b, n):
                def task():
                    if n == 0:
                        wait(e, n_bspill, b, 1)
                    wait(e, n_dbu, b, 4 * (n - 1) if n >= 2 else 4 * (n - 1))
                    src = b_dram[b, n:n + 1, :].broadcast_to([P, TOK])
                    e.dma_start(b_rep[n % 2][:, :], src).then_inc(n_brep[n % 2].sem, 16)
                return task

            def norm(q, b):
                for j in range(TT):
                    def load(j=j):
                        if j < 2:
                            wait(e, n_in, b, 0)
                        elif not isinstance(b, int) or b > 2:
                            wait(e, n_z, b - 2, 0)
                        e.dma_start(x_in[j], x[b, j * P:(j + 1) * P, :]).then_inc(n_xin[j].sem, 16)
                    q.put(NORM[j] - 3, load)

                for i in range(2):
                    def load_w(i=i):
                        wait(e, n_xturn, b, i + 1)
                        e.dma_start(w_xt[i][:, :, :].rearrange("p a b -> p (a b)"), w_in[i]).then_inc(n_wx[i].sem, 16)
                    q.put(NORM[i] + 1.25, load_w)

                def spill():
                    wait(e, n_xnt, b, TT)
                    e.dma_start(xn_dram[b], xnt[:, :, :].rearrange("p a b -> p (a b)")).then_inc(n_xspill.sem, 16)
                q.put(NORM[-1] + 1.99, spill)

            def front(q, b):
                for i in range(DT):
                    def load(i=i):
                        wait(e, n_in, b, i - 1)
                        e.dma_start(w_xt[i % 2][:, :, :].rearrange("p a b -> p (a b)"), w_in[i]).then_inc(n_wx[i % 2].sem, 16)
                    if i >= 2:
                        q.put(X_TILE[i] - 1.5, load)

                    def spill(i=i):
                        wait(e, n_u, b, i + 1)
                        e.dma_start(u_dram[b, i], dtu[:, turn(b), i, :]).then_inc(n_uspill.sem, 16)
                    q.put(X_TILE[i] + AT["x_silu"], spill)

                def spill_b():
                    wait(e, n_xdbl, b, 1)
                    e.dma_start(b_dram[b], xdbl[RANK:RANK + NS, :]).then_inc(n_bspill.sem, 16)
                q.put(X_PROJ + AT["take_xdbl"] - .5, spill_b)

            def back(q, b):
                def load_xn():
                    wait(e, n_xspill, b, 1)
                    wait(e, n_ffn, b, 0)
                    e.dma_start(xnt_b[:, :, :].rearrange("p a b -> p (a b)"), xn_dram[b]).then_inc(n_xback.sem, 16)
                q.put(0, load_xn)
                for i in range(DT):
                    def load(i=i):
                        if i < 2:
                            wait(e, n_xturn, b + 3 if not isinstance(b, int) else min(b + 3, BATCH), 0)
                        else:
                            wait(e, n_z, b, i - 1)
                        e.dma_start(w_zt[i % 2][:, :, :].rearrange("p a b -> p (a b)"), w_in[DT + i]).then_inc(n_wz[i % 2].sem, 16)
                    q.put(max(0, Z_TILE[i] - 1.5), load)

                    def side_u(i=i):
                        if i == 0:
                            wait(e, n_uspill, b, DT)
                            wait(e, n_sum, b, 0)
                        if i >= 2:
                            wait(e, n_y, b, i - 1)
                        e.dma_start(side[i % 2][:, :], u_dram[b, i]).then_inc(n_side[i % 2].sem, 16)
                    q.put(Z_TILE[i] + .25, side_u)
                for j in range(TT):
                    def side_x(j=j):
                        if j < 2:
                            wait(e, n_y, b, DT)
                        else:
                            wait(e, n_sum, b, j - 1)
                        e.dma_start(side[j % 2][:, :], x[b, j * P:(j + 1) * P, :]).then_inc(n_side[j % 2].sem, 16)
                    q.put(OUT[j] + 1, side_x)

                    def store(j=j):
                        wait(e, n_sum, b, j + 1)
                        e.dma_start(out[b, j * P:(j + 1) * P, :], ob[j % 2][:, :]).then_inc(n_store[j % 2].sem, 16)
                    q.put(OUT[j] + AT["residual"] - .5, store)

            loads = [(ident[:, :], ident_in[0]), (ident_had, ident_in[1]),
                     (wx_sb[:, :, :].rearrange("p a b -> p (a b)"), w_x), (wdt_sb[0:RANK, :], w_dt), (a_sb[:, :], a_log),
                     (cw[:, :], conv_w), (ch[:, :, :].rearrange("p a b -> p (a b)"), chan), (bias_sb, bias)]
            assert len(loads) == LOADS
            for to, src in loads:
                e.dma_start(to, src).then_inc(p_load.sem, 16)
            q = Slots()
            norm(q, 0)
            spill = q.at.pop(NORM[-1] + 1)
            for s in range(LAST):
                q.run(s, [])
            for i in range(2):
                e.dma_start(acc[:, i * HALF:(i + 1) * HALF, :, :].rearrange("p d a b -> p (d a b)"),
                            w_out[:, i * HALF * DM:(i + 1) * HALF * DM]).then_inc(p_wout.sem, 16)
            for _, task in spill:
                task()
            for r in range(5):
                e.dma_start(f_slot(r), factors[r].rearrange("p (a b) -> p a b", a=KT)).then_inc(p_f[r].sem, 16)
            q = Slots()
            front(q, 0)
            norm(q, 1)
            for s in range(LAST):
                q.run(s, [])
            for r in range(5, FACTORS):
                wait(e, p_fadd, 0, r - 4)
                e.dma_start(f_slot(r), factors[r].rearrange("p (a b) -> p a b", a=KT)).then_inc(p_f[r].sem, 16)
            b_load(0, 0)()

            def round_(t, has_front, has_norm, has_back):
                q = fill(t, has_front, has_norm, has_back, front, norm, back)
                for n in range(1, NS):
                    q.put(max(0, 2 * n - 2.5), b_load(t, n))
                if has_front:
                    q.put(STEPS - .1, b_load(t + 1, 0))
                for s in range(STEPS):
                    q.run(s, [])

            rounds(e, round_)
            q = fill(BATCH, False, False, True, None, None, back)
            for s in range(LAST):
                q.run(s, [])
            for i in range(2):
                wait(e, n_store[i], BATCH - 1, TT // 2)


def kernel(**inputs):
    from concourse import bacc
    from concourse.bass_utils import run_bass_kernel_spmd

    a = {k.removeprefix("L0_attn_"): np.asarray(v) for k, v in inputs.items()}

    def tiles(v, n):
        return np.ascontiguousarray(v.reshape(n, P, -1).transpose(1, 0, 2).reshape(P, -1))

    h = np.array([[1.0]])
    while h.shape[0] < P:
        h = np.block([[h, h], [h, -h]])
    had = (h / (4 * DI ** 0.5)).astype(np.float32)
    w_in = a["W_in"]
    arrays = {
        "x": a["hidden_states"],
        "w_in": np.ascontiguousarray(w_in.reshape(2 * DT, P, KT, P).transpose(0, 3, 2, 1).reshape(2 * DT, P, KT * P)),
        "w_x": tiles(a["W_x"].T, DT),
        "w_dt": np.ascontiguousarray(a["W_dt"].T),
        "w_out": tiles(a["W_out"].T, DT),
        "a_log": tiles(a["A_log"], DT),
        "conv_w": tiles(a["conv_w"], DT),
        "chan": np.concatenate([tiles(a[n].reshape(-1, 1), DT) for n in ("conv_b", "dt_bias", "D")], axis=1),
        "factors": np.ascontiguousarray(a["L0_ffn_factors"].reshape(FACTORS, KT, P, DM).transpose(0, 2, 1, 3)
                                        .reshape(FACTORS, P, KT * DM)),
        "bias": a["L0_ffn_bias"].reshape(1, DM),
        "consts": np.stack([np.eye(P, dtype=np.float32), had]),
    }
    nc = bacc.Bacc("TRN2", target_bir_lowering=False, num_devices=1)
    ap = {n: nc.dram_tensor(f"in_{n}", v.shape, F32, kind="ExternalInput").ap() for n, v in arrays.items()}
    u_dram = nc.dram_tensor("u_dram", [BATCH, DT, P, TOK], F32, kind="Internal").ap()
    xn_dram = nc.dram_tensor("xn_dram", [BATCH, P, KT * TOK], F32, kind="Internal").ap()
    b_dram = nc.dram_tensor("b_dram", [BATCH, NS, TOK], F32, kind="Internal").ap()
    out = nc.dram_tensor("out", [BATCH, TOK, DM], F32, kind="ExternalOutput").ap()
    program(nc, ap["x"], ap["w_in"], ap["w_x"], ap["w_dt"], ap["w_out"], ap["a_log"], ap["conv_w"], ap["chan"],
            ap["factors"], ap["bias"], None, ap["consts"], u_dram, xn_dram, b_dram, out)
    r = run_bass_kernel_spmd(nc, [{f"in_{n}": v for n, v in arrays.items()}], core_ids=[0])
    return r.results[0]["out"]
```

```python
from contextlib import ExitStack

import numpy as np

import concourse.bass as bass
from concourse import mybir

F32 = mybir.dt.float32
ALU = mybir.AluOpType
ACT = mybir.ActivationFunctionType

APART = (mybir.EngineType.Activation, mybir.EngineType.Pool, mybir.EngineType.SP)
P = 128
BATCH, TOK, DM = 16, 512, 512
DI = 2 * DM
NS = 16
TAPS = 4
RANK = DM // 16
FACTORS = 8
KT = DM // P
DT = DI // P
TT = TOK // P
HALF = DT // 2
STEPS = 2 * NS
SCANS = HALF * STEPS
MACS = TT * STEPS
NX = RANK + 2 * NS
EPS = 1e-5

X_TILE = [1 + 2 * i for i in range(DT)]
X_PROJ = 17
DT_TILE = [20.125 + i for i in range(DT)]
NORM = [28 + i for i in range(TT)]
Z_TILE = [2 * i for i in range(DT)]
FFN = [15.75, 17.25, 18.5, 19.75]
OUT = [21.25, 23.25, 25.5, 27.5]
AHEAD = DT + TT
AHEAD_AT = X_TILE + [20.5 + 2.5 * j for j in range(TT)]
AT = {
    "x_tile": (0.375, 0.75, 1, 1),
    "tap": (1.75, 1.5, 1.875, 2),
    "x_tanh": 3,
    "x_plus": 3.25,
    "x_silu": 4,
    "x_proj": (0.5, 0.5, 0.5, 1, 1.5, 1.5, 2, 2),
    "take_xdbl": 3.25,
    "c_turn": 3,
    "take_c": 3.25,
    "dt_tile": 1,
    "relu": 2,
    "sp_exp": 2.5,
    "sp_ln": 2.75,
    "sp_add": 3,
    "dtu": 3,
    "stats": (-1.75, -1.5, -1.25),
    "rstd": -0.5,
    "shift": -0.625,
    "normalise": 0.5,
    "n_turn": 1,
    "xnt": 2,
    "z_tile": (0.75, 0.75, 1, 1.25),
    "z_tanh": 2,
    "z_silu": 1.875,
    "y_turn": 2.125,
    "scale_u": 1.5,
    "take_y": 3,
    "skip": 3.25,
    "gate": 4,
    "ffn": (0.5, 0.75, 1, 1.25),
    "f_tanh": 2,
    "f_silu": 1.375,
    "out": (0.25, 0.5, 0.75, 1, 1.25, 1.5, 1.75, 2),
    "out_gate": 2.5,
    "residual": 3.5,
}
LN_TABLE, TANH_TABLE = 22.375, 31
LAST = 36


class Count:

    def __init__(self, sem, per, unit, waited):
        self.sem, self.per, self.unit, self.waited = sem, per, unit, waited

    def upto(self, batch, n):
        if isinstance(batch, int):
            return (batch * self.per + n) * self.unit
        return batch * (self.per * self.unit) + n * self.unit


def wait(e, count, batch, n, apart=False):
    value = count.upto(batch, n)
    if not isinstance(value, int) or value > 0:
        e.wait_ge(count.sem, value)
        if not isinstance(value, int) and (apart or e.engine in APART):
            e.sem_inc(count.waited, 1)


class Slots:

    def __init__(self, end=None):
        self.at, self.end, self.late = {}, end, False

    def put(self, time, task):
        if self.end is not None:
            if (time >= self.end) != self.late:
                return
            time -= self.end * self.late
        step = int(time)
        self.at.setdefault(step, []).append((time - step, task))

    def run(self, step, own):
        extra = sorted(self.at.get(step, []), key=lambda x: x[0])
        for i, instruction in enumerate(own):
            while extra and extra[0][0] * len(own) <= i:
                extra.pop(0)[1]()
            instruction()
        for _, task in extra:
            task()


def program(nc, x, w_in, w_x, w_dt, w_out, a_log, conv_w, chan, factors, bias, consts,
            u_dram, xn_dram, b_dram, out):
    ctx = ExitStack()
    with ctx:
        def sb(name, shape):
            return ctx.enter_context(nc.sbuf_tensor(name, shape, F32))

        def ps(name, shape):
            return ctx.enter_context(nc.psum_tensor(name, shape, F32))

        waited = ctx.enter_context(nc.semaphore("waited"))

        def count(name, per, unit=1):
            return Count(ctx.enter_context(nc.semaphore(name)), per, unit, waited)

        wx_sb = sb("wx_sb", [P, DT, NX])
        wdt_sb = sb("wdt_sb", [RANK + 1, DI])
        wc_sb = sb("wc_sb", [P, DT, DM])
        f_sb = sb("f_sb", [P, KT, DM])
        ident = sb("ident", [P, P])
        a_sb = sb("a_sb", [P, DT * NS])
        cw = sb("cw", [P, DT * TAPS])
        ch = sb("ch", [P, 3, DT])
        bias_sb = wdt_sb[RANK:RANK + 1, 0:DM]
        ones = wdt_sb[RANK:RANK + 1, DM:DM + P]
        w_xt = [sb(f"w_xt{i}", [P, KT, P]) for i in range(2)]
        w_zt = [sb(f"w_zt{i}", [P, KT, P]) for i in range(2)]
        delta = sb("delta", [P, 2, DT, TOK])
        dtu = sb("dtu", [P, 2, DT, TOK])
        acc = sb("acc", [P, DT, TT, P])
        acc_f = sb("acc_f", [P, DT, TT, P])
        h = [sb(f"h{i}", [P, HALF, TOK]) for i in range(2)]
        dbu = [sb(f"dbu{i}", [P, 2, TOK]) for i in range(2)]
        b_rep = [sb(f"b_rep{i}", [P, TOK]) for i in range(2)]
        c_now = sb("c_now", [P, TT, NS])
        c_next = sb("c_next", [P, TT, NS])
        xnt = sb("xnt", [P, KT, TOK])
        xnt_b = sb("xnt_b", [P, KT, TOK])
        x_in = [buf[:, :, :].rearrange("p a b -> p (a b)") for buf in w_xt + w_zt]
        stats = sb("stats", [P, 2, 6])
        mv = sb("mv", [P, 2, 2])
        rs = sb("rs", [P, 2, 2])
        power = sb("power", [P, 1])
        side = [sb(f"side{i}", [P, TOK]) for i in range(2)]
        sp = [sb(f"sp{i}", [P, TOK]) for i in range(2)]
        sz = sb("sz", [P, TOK])
        yb = sb("yb", [P, TOK])
        ob = [sz, yb]
        ident_had = sz[:, 0:P]
        gf = sb("gf", [P, TT, DM])
        xdbl = sb("xdbl", [NX, TOK])

        decay = [ps(f"decay{i}", [P, TOK]) for i in range(3)]
        ht = [ps(f"ht{i}", [P, HALF, P]) for i in range(2)]
        pf = ps("pf", [P, TOK])
        pb = ps("pb", [P, TOK])
        px = ps("px", [P, TOK])
        back_bank = [pb, px]

        n_decay = count("n_decay", SCANS)
        n_dbu = count("n_dbu", SCANS // 2)
        n_scan = count("n_scan", SCANS)
        n_ht = count("n_ht", MACS)
        n_mac = count("n_mac", MACS)
        n_brep = [count(f"n_brep{i}", NS // 2, 16) for i in range(2)]
        n_xin = [count(f"n_xin{j}", 1, 16) for j in range(TT)]
        n_stat = count("n_stat", 3 * TT)
        n_shift = count("n_shift", TT)
        n_rstd = count("n_rstd", TT)
        n_norm = count("n_norm", TT)
        n_xturn = count("n_xturn", TT)
        n_xnt = count("n_xnt", TT)
        n_xspill = count("n_xspill", 1, 16)
        n_wx = [count(f"n_wx{i}", DT // 2, 16) for i in range(2)]
        n_in = count("n_in", DT)
        n_tap0 = count("n_tap0", DT)
        n_tap = count("n_tap", DT * (TAPS - 1))
        n_tanh = count("n_tanh", DT)
        n_plus = count("n_plus", DT)
        n_u = count("n_u", DT)
        n_uspill = count("n_uspill", DT, 16)
        n_xproj = count("n_xproj", 1)
        n_xdbl = count("n_xdbl", 1)
        n_bspill = count("n_bspill", 1, 16)
        n_cturn = count("n_cturn", 1)
        n_cnext = count("n_cnext", 1)
        n_cnow = count("n_cnow", 1)
        n_dt = count("n_dt", DT)
        n_relu = count("n_relu", DT)
        n_abs = count("n_abs", DT)
        n_exp = count("n_exp", DT)
        n_ln = count("n_ln", DT)
        n_delta = count("n_delta", DT)
        n_dtu = count("n_dtu", DT)
        n_xback = count("n_xback", 1, 16)
        n_wz = [count(f"n_wz{i}", DT // 2, 16) for i in range(2)]
        n_z = count("n_z", DT)
        n_ztanh = count("n_ztanh", DT)
        n_sz = count("n_sz", DT)
        n_side = [count(f"n_side{i}", (DT + TT) // 2, 16) for i in range(2)]
        n_yturn = count("n_yturn", DT)
        n_du = count("n_du", DT)
        n_skip = count("n_skip", DT)
        n_y = count("n_y", DT)
        n_g = count("n_g", DT)
        n_ffn = count("n_ffn", TT)
        n_ftanh = count("n_ftanh", TT)
        n_gf = count("n_gf", TT)
        n_out = count("n_out", TT)
        n_o = count("n_o", TT)
        n_sum = count("n_sum", TT)
        n_store = [count(f"n_store{i}", TT // 2, 16) for i in range(2)]
        n_aload = [count(f"n_aload{i}", DT // 2, 16) for i in range(2)]
        n_a = count("n_a", AHEAD)
        n_atanh = count("n_atanh", AHEAD)
        n_asilu = count("n_asilu", AHEAD)
        p_load = count("p_load", 1, 16)
        p_wout = count("p_wout", 1, 16)
        p_f = [count(f"p_f{i}", 1, 16) for i in range(FACTORS)]
        p_fadd = count("p_fadd", 1)
        p_fscale = count("p_fscale", 1)
        p_act = count("p_act", 1)
        p_dve = count("p_dve", 1)
        p_h = count("p_h", 1)
        p_hcopy = count("p_hcopy", 1)
        p_fold = count("p_fold", 1)

        LOADS = 8

        f_part = ([f_sb[:, :, :]] + [buf[:, 1, i * KT:(i + 1) * KT, :] for buf in (delta, dtu) for i in range(2)]
                  + [gf[:, :, :], h[0][:, :, :], h[1][:, :, :]])

        def turn(b):
            return b % 2

        def first(b):
            return isinstance(b, int) and b == 0

        def final(b):
            return isinstance(b, int) and b == BATCH - 1

        def x_bank(b, i):
            return px if first(b) and i % 2 else pf

        def y_bank(b, i):
            return pf if final(b) and i % 2 else pb

        def z_of(b, i):
            return delta[:, turn(b + 1), i, :] if final(b) else sz[:, :]

        def f_of(b, j):
            return dtu[:, turn(b + 1), j, :] if final(b) else gf[:, j, :]

        def ahead_to(i):
            return z_of(BATCH - 1, i) if i < DT else f_of(BATCH - 1, i - DT)

        block = ctx.enter_context(nc.Block())

        def fill(t, has_front, has_norm, has_back, front, norm, back, ahead):
            q = Slots(STEPS if not isinstance(t, int) or t < BATCH else LAST)
            if has_front:
                front(q, t + 1)
            if has_norm:
                norm(q, t + 2)
            if has_back:
                back(q, t - 1)
            q.late, q.end = True, STEPS
            if not isinstance(t, int) or 0 < t < BATCH:
                front(q, t)
            if not isinstance(t, int) or 0 < t < BATCH - 1:
                norm(q, t + 1)
            if not isinstance(t, int) or t > 1:
                back(q, t - 2)
            q.late = False
            if final(t):
                ahead(q)
            return q

        def rounds(e, round_):
            round_(0, True, True, False)
            round_(1, True, True, True)
            with e.Fori(2, BATCH - 2) as t:
                round_(t, True, True, True)
            round_(BATCH - 2, True, False, True)
            round_(BATCH - 1, False, False, True)

        @block.tensor
        def _(e):
            def turns(b, s, j):
                def task():
                    wait(e, n_scan, b, HALF * (s + 1))
                    wait(e, n_mac, b, TT * s + j - 1)
                    for i in range(HALF):
                        mm = e.transpose(ht[j % 2][:, i, :], h[s % 2][:, i, j * P:(j + 1) * P], ident[:, :])
                    mm.then_inc(n_ht.sem, 1)
                return task

            def norm(q, b):
                for j in range(TT):
                    def task(j=j):
                        wait(e, n_norm, b, j + 1)
                        if j == 0:
                            wait(e, n_abs, b, 0)
                        else:
                            wait(e, n_xnt, b, j)
                        for k in range(KT):
                            mm = e.transpose(pf[:, k * P:(k + 1) * P], x_in[j][:, k * P:(k + 1) * P], ident[:, :])
                        mm.then_inc(n_xturn.sem, 1)
                    q.put(NORM[j] + AT["n_turn"], task)

            def front(q, b):
                for i in range(DT):
                    def x_tile(k, i=i):
                        if k == 0:
                            wait(e, n_xnt, b, TT)
                            wait(e, n_tap, b, (TAPS - 1) * (i - first(b)))
                            wait(e, n_wx[i % 2], b, i // 2 + 1)
                        mm = e.matmul(x_bank(b, i)[:, :], w_xt[i % 2][:, k, :], xnt[:, k, :], start=k == 0, stop=k == KT - 1)
                        if k == KT - 1:
                            mm.then_inc(n_in.sem, 1)
                    for k in range(KT):
                        q.put(X_TILE[i] + AT["x_tile"][k], lambda k=k, f=x_tile: f(k))

                def x_proj(i):
                    if i == 0:
                        wait(e, n_tap, b, (TAPS - 1) * DT)
                    wait(e, n_u, b, i + 1)
                    mm = e.matmul(pf[0:NX, :], wx_sb[:, i, :], dtu[:, turn(b), i, :], start=i == 0, stop=i == DT - 1)
                    if i == DT - 1:
                        mm.then_inc(n_xproj.sem, 1)
                for i in range(DT):
                    q.put(X_PROJ + AT["x_proj"][i], lambda i=i: x_proj(i))

                def c_turn():
                    wait(e, n_xdbl, b, 1, apart=True)
                    for j in range(TT):
                        mm = e.transpose(pf[:, j * NX:(j + 1) * NX], xdbl[:, j * P:(j + 1) * P], ident[0:NX, 0:NX])
                    mm.then_inc(n_cturn.sem, 1)
                q.put(X_PROJ + AT["c_turn"], c_turn)

                for i in range(DT):
                    def dt_tile(i=i):
                        if i == 0:
                            wait(e, n_cnext, b, 1)
                        else:
                            wait(e, n_abs, b, i - first(b))
                            wait(e, n_relu, b, i - first(b))
                        e.matmul(x_bank(b, i)[:, :], wdt_sb[0:RANK, i * P:(i + 1) * P], xdbl[0:RANK, :],
                                 start=True, stop=True).then_inc(n_dt.sem, 1)
                    q.put(DT_TILE[i] + AT["dt_tile"], dt_tile)

            def back(q, b):
                for i in range(DT):
                    def z_tile(k, i=i):
                        if k == 0:
                            wait(e, n_xback, b, 1)
                            if i == 0:
                                wait(e, n_o, b, 0)
                            else:
                                wait(e, n_y, b, i)
                            wait(e, n_wz[i % 2], b, i // 2 + 1)
                        mm = e.matmul(pb[:, :], w_zt[i % 2][:, k, :], xnt_b[:, k, :], start=k == 0, stop=k == KT - 1)
                        if k == KT - 1:
                            mm.then_inc(n_z.sem, 1)
                    for k in range(KT if not final(b) else 0):
                        q.put(Z_TILE[i] + AT["z_tile"][k], lambda k=k, f=z_tile: f(k))

                    def y_turn(i=i):
                        wait(e, n_mac, b, MACS)
                        if final(b):
                            wait(e, n_o, b, 0)
                            wait(e, n_asilu, 0, AHEAD)
                            wait(e, n_y, b, i - 1)
                        else:
                            wait(e, n_sz, b, i + 1)
                        for j in range(TT):
                            mm = e.transpose(y_bank(b, i)[:, j * P:(j + 1) * P], acc_f[:, i, j, :], ident[:, :])
                        mm.then_inc(n_yturn.sem, 1)
                    q.put(Z_TILE[i] + AT["y_turn"], y_turn)

                for j in range(TT):
                    def ffn(k, j=j):
                        if k == 0:
                            if j == 0:
                                wait(e, n_xback, b, 1)
                                wait(e, n_o, b, 0)
                            else:
                                wait(e, n_gf, b, j)
                        e.matmul(px[:, :], xnt_b[:, k, j * P:(j + 1) * P], f_sb[:, k, :], start=k == 0, stop=False)
                        if k == KT - 1:
                            e.matmul(px[:, :], ones, bias_sb, start=False, stop=True).then_inc(n_ffn.sem, 1)
                    for k in range(KT if not final(b) else 0):
                        q.put(FFN[j] + AT["ffn"][k], lambda k=k, f=ffn: f(k))

                    def out_tile(i, j=j):
                        if i == 0:
                            wait(e, n_g, b, DT)
                            if j < 2:
                                wait(e, n_y if final(b) or j == 0 else n_gf, b, DT if final(b) or j == 0 else TT)
                            else:
                                wait(e, n_o, b, j - 1)
                        g = acc_f[:, i, :, :].rearrange("p a b -> p (a b)")
                        mm = e.matmul(back_bank[j % 2][:, :], g[:, j * P:(j + 1) * P], wc_sb[:, i, :],
                                      start=i == 0, stop=i == DT - 1)
                        if i == DT - 1:
                            mm.then_inc(n_out.sem, 1)
                    for i in range(DT):
                        q.put(OUT[j] + AT["out"][i], lambda i=i, f=out_tile: f(i))

            def ahead(q):
                for i in range(AHEAD):
                    def tile(k, i=i):
                        if k == 0:
                            if i == 0:
                                wait(e, n_relu, BATCH, 0)
                                wait(e, n_abs, BATCH, 0)
                            else:
                                wait(e, n_asilu, 0, i)
                            if i < DT:
                                wait(e, n_aload[i % 2], 0, i // 2 + 1)
                        if i < DT:
                            mm = e.matmul(pf[:, :], w_xt[i % 2][:, k, :], xnt[:, k, :], start=k == 0, stop=k == KT - 1)
                        else:
                            j = i - DT
                            mm = e.matmul(pf[:, :], xnt[:, k, j * P:(j + 1) * P], f_sb[:, k, :], start=k == 0, stop=False)
                            if k == KT - 1:
                                mm = e.matmul(pf[:, :], ones, bias_sb, start=False, stop=True)
                        if k == KT - 1:
                            mm.then_inc(n_a.sem, 1)
                    for k in range(KT):
                        q.put(AHEAD_AT[i] + AT["z_tile"][k], lambda k=k, f=tile: f(k))

            wait(e, p_load, 0, LOADS)
            q = Slots()
            norm(q, 0)
            for s in range(LAST):
                q.run(s, [])
            wait(e, p_wout, 0, 2)
            for i in range(DT):
                bank = (decay + [pb])[i % 4][:, :]
                if i >= 4:
                    wait(e, p_hcopy, 0, i - 3)
                e.matmul(bank, ident_had, acc[:, i, :, :].rearrange("p a b -> p (a b)"),
                         start=True, stop=True).then_inc(p_h.sem, 1)
            q = Slots()
            front(q, 0)
            norm(q, 1)
            for s in range(LAST):
                q.run(s, [])

            def round_(t, has_front, has_norm, has_back):
                q = fill(t, has_front, has_norm, has_back, front, norm, back, ahead)
                for s in range(STEPS):
                    if s == 0:
                        own = [turns(t - 1, STEPS - 1, j) for j in range(TT)] if has_back else []
                    else:
                        own = [turns(t, s - 1, j) for j in range(TT)]
                    q.run(s, own)

            wait(e, p_fold, 0, 24)
            wait(e, p_fscale, 0, 1)
            rounds(e, round_)
            for j in range(TT):
                turns(BATCH - 1, STEPS - 1, j)()
            q = fill(BATCH, False, False, True, None, None, back, None)
            for s in range(LAST):
                q.run(s, [])

        @block.scalar
        def _(e):
            def decays(b, s, i):
                q, tile = HALF * s + i, HALF * (s % 2) + i

                def task():
                    if s == 0 and i == 0:
                        wait(e, n_delta, b, DT)
                    wait(e, n_scan, b, q - 2 if q >= 2 else q - 1)
                    n = tile * NS + s // 2
                    e.activation(decay[q % 3][:, :], delta[:, turn(b), tile, :], ACT.Exp,
                                 bias=0.0, scale=a_sb[:, n:n + 1]).then_inc(n_decay.sem, 1)
                return task

            def norm(q, b):
                for j in range(TT):
                    def normalise(j=j):
                        wait(e, n_shift, b, j + 1)
                        e.activation(x_in[j], x_in[j], ACT.Identity, bias=rs[:, j % 2, 1:2],
                                     scale=rs[:, j % 2, 0:1]).then_inc(n_norm.sem, 1)
                    q.put(NORM[j] + AT["normalise"], normalise)

                    def evacuate(j=j):
                        wait(e, n_xturn, b, j + 1)
                        if j == 0:
                            wait(e, n_in, b, 0)
                            wait(e, n_xspill, b, 0)
                        e.copy(xnt[:, :, j * P:(j + 1) * P],
                               pf[:, :].rearrange("p (k b) -> p k b", k=KT)).then_inc(n_xnt.sem, 1)
                    q.put(NORM[j] + AT["xnt"], evacuate)

            def front(q, b):
                for i in range(DT):
                    def tap0(i=i):
                        if i == 0:
                            wait(e, n_dbu, b - 1, 0) if not isinstance(b, int) or b >= 1 else None
                        wait(e, n_in, b, i + 1)
                        k = i * TAPS + TAPS - 1
                        e.activation(dtu[:, turn(b), i, :], x_bank(b, i)[:, :], ACT.Identity, bias=ch[:, 0, i:i + 1],
                                     scale=cw[:, k:k + 1]).then_inc(n_tap0.sem, 1)
                    q.put(X_TILE[i] + AT["tap"][0], tap0)

                    def tanh(i=i):
                        wait(e, n_tap, b, (TAPS - 1) * (i + 1))
                        wait(e, n_u, b, i)
                        if i == 0:
                            wait(e, n_delta, b, 0)
                        e.activation(sp[1][:, :], dtu[:, turn(b), i, :], ACT.Tanh).then_inc(n_tanh.sem, 1)
                    q.put(X_TILE[i] + AT["x_tanh"], tanh)

                    def plus_one(i=i):
                        wait(e, n_tanh, b, i + 1)
                        e.activation(sp[1][:, :], sp[1][:, :], ACT.Identity, bias=1.0, scale=1.0).then_inc(n_plus.sem, 1)
                    q.put(X_TILE[i] + AT["x_plus"], plus_one)

                def take_xdbl():
                    wait(e, n_xproj, b, 1)
                    wait(e, n_dt, b, 0)
                    wait(e, n_bspill, b, 0)
                    e.copy(xdbl[:, :], pf[0:NX, :]).then_inc(n_xdbl.sem, 1)
                q.put(X_PROJ + AT["take_xdbl"], take_xdbl)

                for i in range(DT):
                    def relu(i=i):
                        wait(e, n_dt, b, i + 1)
                        e.activation(delta[:, turn(b), i, :], x_bank(b, i)[:, :], ACT.Relu, bias=ch[:, 1, i:i + 1],
                                     scale=1.0).then_inc(n_relu.sem, 1)
                        if i >= 2:
                            wait(e, n_delta, b, i - 1)
                        elif i == 1 and not (isinstance(b, int) and b < 2):
                            wait(e, n_sz, b - 1, 0)
                        e.activation(sp[(i + 1) % 2][:, :], x_bank(b, i)[:, :], ACT.Abs, bias=ch[:, 1, i:i + 1],
                                     scale=1.0).then_inc(n_abs.sem, 1)
                    q.put(DT_TILE[i] + AT["relu"], relu)

                    def exp(i=i):
                        wait(e, n_abs, b, i + 1)
                        e.activation(sp[(i + 1) % 2][:, :], sp[(i + 1) % 2][:, :], ACT.Exp,
                                     scale=-1.0).then_inc(n_exp.sem, 1)
                    q.put(DT_TILE[i] + AT["sp_exp"], exp)

                    def ln(i=i):
                        wait(e, n_exp, b, i + 1)
                        e.activation(sp[(i + 1) % 2][:, :], sp[(i + 1) % 2][:, :], ACT.Ln, bias=1.0).then_inc(n_ln.sem, 1)
                    q.put(DT_TILE[i] + AT["sp_ln"], ln)
                q.put(LN_TABLE, lambda: e.preload_act_table_set("natural_log_exp_and_others"))
                q.put(TANH_TABLE, lambda: e.preload_act_table_set("exp_and_others"))

            def back(q, b):
                if final(b):
                    return
                for i in range(DT):
                    def z_tanh(i=i):
                        if i == 0:
                            wait(e, n_delta, b + 1, DT) if not isinstance(b, int) or b < BATCH - 1 else None
                        wait(e, n_z, b, i + 1)
                        e.activation(sp[0][:, :], pb[:, :], ACT.Tanh, scale=0.5).then_inc(n_ztanh.sem, 1)
                    q.put(Z_TILE[i] + AT["z_tanh"], z_tanh)
                for i in range(DT):
                    def scale_u(i=i):
                        wait(e, n_side[i % 2], b, i // 2 + 1)
                        e.activation(side[i % 2][:, :], side[i % 2][:, :], ACT.Identity, bias=0.0,
                                     scale=ch[:, 2, i:i + 1]).then_inc(n_du.sem, 1)
                    q.put(Z_TILE[i] + AT["scale_u"], scale_u)

                    def take_y(i=i):
                        wait(e, n_yturn, b, i + 1)
                        wait(e, n_g, b, i)
                        if i == 0:
                            wait(e, n_store[1], b, 0)
                        e.copy(yb[:, :], y_bank(b, i)[:, :]).then_inc(n_y.sem, 1)
                    q.put(Z_TILE[i] + AT["take_y"], take_y)
                for j in range(TT):
                    def f_tanh(j=j):
                        wait(e, n_ffn, b, j + 1)
                        wait(e, n_o, b, 0)
                        e.activation(gf[:, j, :], px[:, :], ACT.Tanh, scale=0.5).then_inc(n_ftanh.sem, 1)
                    q.put(FFN[j] + AT["f_tanh"], f_tanh)

            def ahead(q):
                for i in range(AHEAD):
                    def tanh(i=i):
                        wait(e, n_a, 0, i + 1)
                        if i == 0:
                            wait(e, n_delta, BATCH, 0)
                        else:
                            wait(e, n_asilu, 0, i)
                        e.activation(sp[1][:, :], pf[:, :], ACT.Tanh, scale=0.5).then_inc(n_atanh.sem, 1)
                    q.put(AHEAD_AT[i] + AT["z_tanh"] + (i >= DT) / 2, tanh)

            wait(e, p_load, 0, LOADS)
            e.activation(a_sb[:, :], a_sb[:, :], ACT.Exp).then_inc(p_act.sem, 1)
            e.mul(cw[:, :], cw[:, :], 0.5).then_inc(p_act.sem, 1)
            e.mul(ch[:, 0, :], ch[:, 0, :], 0.5).then_inc(p_act.sem, 1)
            wait(e, p_act, 0, 1)
            e.mul(a_sb[:, :], a_sb[:, :], -1.0).then_inc(p_act.sem, 1)
            wait(e, p_act, 0, 4)
            q = Slots()
            norm(q, 0)
            for s in range(LAST):
                q.run(s, [])
            for i in range(DT):
                bank = (decay + [pb])[i % 4][:, :]
                wait(e, p_h, 0, i + 1)
                e.copy(acc_f[:, i, :, :], bank.rearrange("p (a b) -> p a b", a=TT)).then_inc(p_hcopy.sem, 1)
            q = Slots()
            front(q, 0)
            norm(q, 1)

            def scale_f():
                wait(e, p_fadd, 0, FACTORS - 1)
                e.mul(f_sb[:, :, :], f_sb[:, :, :], FACTORS ** -0.5).then_inc(p_fscale.sem, 1)
            q.put(X_PROJ + 4, scale_f)
            for s in range(LAST):
                q.run(s, [])

            def round_(t, has_front, has_norm, has_back):
                q = fill(t, has_front, has_norm, has_back, front, norm, back, ahead)
                for s in range(STEPS):
                    q.run(s, [decays(t, s, i) for i in range(HALF)])

            rounds(e, round_)
            q = fill(BATCH, False, False, True, None, None, back, None)
            for s in range(LAST):
                q.run(s, [])

        @block.gpsimd
        def _(e):
            def inputs(b, s, p):
                q, tile = 2 * s + p, HALF * (s % 2) + 2 * p
                n = s // 2

                def task():
                    if s == 0 and p == 0:
                        wait(e, n_dtu, b, DT)
                    wait(e, n_brep[n % 2], b, n // 2 + 1)
                    wait(e, n_scan, b, 2 * (q - 1))
                    e.tensor_tensor(dbu[q % 2][:, :, :], dtu[:, turn(b), tile:tile + 2, :],
                                    b_rep[n % 2][:, None, :].broadcast_to([P, 2, TOK]), ALU.mult).then_inc(n_dbu.sem, 1)
                return task

            def front(q, b):
                for i in range(DT):
                    def silu(i=i):
                        wait(e, n_plus, b, i + 1)
                        e.tensor_tensor(dtu[:, turn(b), i, :], dtu[:, turn(b), i, :], sp[1][:, :],
                                        ALU.mult).then_inc(n_u.sem, 1)
                    q.put(X_TILE[i] + AT["x_silu"], silu)

                    def add(i=i):
                        wait(e, n_ln, b, i + 1)
                        e.tensor_tensor(delta[:, turn(b), i, :], delta[:, turn(b), i, :], sp[(i + 1) % 2][:, :],
                                        ALU.add).then_inc(n_delta.sem, 1)
                    q.put(DT_TILE[i] + AT["sp_add"], add)


            def back(q, b):
                for i in range(DT if not final(b) else 0):
                    def skip(i=i):
                        wait(e, n_y, b, i + 1)
                        wait(e, n_du, b, i + 1)
                        e.tensor_tensor(yb[:, :], yb[:, :], side[i % 2][:, :], ALU.add).then_inc(n_skip.sem, 1)
                    q.put(Z_TILE[i] + AT["skip"], skip)

                    def gate(i=i):
                        wait(e, n_skip, b, i + 1)
                        wait(e, n_sz, b, i + 1)
                        e.tensor_tensor(acc_f[:, i, :, :].rearrange("p a b -> p (a b)"), yb[:, :], sz[:, :],
                                        ALU.mult).then_inc(n_g.sem, 1)
                    q.put(Z_TILE[i] + AT["gate"], gate)
                for j in range(TT):
                    def residual(j=j):
                        wait(e, n_o, b, j + 1)
                        wait(e, n_side[j % 2], b, (DT + j) // 2 + 1)
                        e.tensor_tensor(ob[j % 2][:, :], ob[j % 2][:, :], side[j % 2][:, :],
                                        ALU.add).then_inc(n_sum.sem, 1)
                    q.put(OUT[j] + AT["residual"], residual)

            def ahead(q):
                pass

            def norm(q, b):
                for j in range(TT):
                    def rstd(j=j, r=j % 2):
                        wait(e, n_stat, b, 3 * j + 3)
                        if j >= 2:
                            wait(e, n_norm, b, j - 1)
                        else:
                            wait(e, n_norm, b, 0)
                        e.tensor_tensor(rs[:, r, 0:1], mv[:, r, 1:2], power[:, :], ALU.pow).then_inc(n_rstd.sem, 1)
                    q.put(NORM[j] + AT["rstd"], rstd)

            wait(e, p_dve, 0, 1)
            q = Slots()
            norm(q, 0)
            for s in range(LAST):
                q.run(s, [])
            q = Slots()
            front(q, 0)
            norm(q, 1)
            for s in range(LAST):
                q.run(s, [])

            def round_(t, has_front, has_norm, has_back):
                q = fill(t, has_front, has_norm, has_back, front, norm, back, ahead)
                for s in range(STEPS):
                    q.run(s, [inputs(t, s, p) for p in range(2)])

            rounds(e, round_)
            q = fill(BATCH, False, False, True, None, None, back, None)
            for s in range(LAST):
                q.run(s, [])

        @block.vector
        def _(e):
            def scan(b, s, i):
                q = HALF * s + i

                def task():
                    wait(e, n_decay, b, q + 1)
                    if i % 2 == 0:
                        wait(e, n_dbu, b, q // 2 + 1)
                    e.tensor_tensor_scan(h[s % 2][:, i, :], decay[q % 3][:, :], dbu[q // 2 % 2][:, i % 2, :],
                                         0.0, ALU.mult, ALU.add).then_inc(n_scan.sem, 1)
                return task

            def mac(b, s, j):
                n, half = s // 2, s % 2

                def task():
                    tiles = slice(half * HALF, (half + 1) * HALF)
                    wait(e, n_ht, b, TT * s + j + 1)
                    if s == 0 and j == 0:
                        wait(e, n_cnow, b, 1)
                    c = c_now[:, j, n:n + 1]
                    if n == 0:
                        op = e.tensor_scalar(acc[:, tiles, j, :], ht[j % 2][:, :, :], c, None, ALU.mult)
                    else:
                        wait(e, n_mac, b, TT * (s - 2) + j + 1)
                        if n == NS - 1 and half == 0 and j == 0:
                            wait(e, n_out, b, 0)
                        to = acc_f if n == NS - 1 else acc
                        op = e.scalar_tensor_tensor(out=to[:, tiles, j, :], in0=ht[j % 2][:, :, :], scalar=c,
                                                    in1=acc[:, tiles, j, :], op0=ALU.mult, op1=ALU.add)
                    op.then_inc(n_mac.sem, 1)
                return task

            def norm(q, b):
                for j in range(TT):
                    r = j % 2

                    def bn(j=j, r=r):
                        wait(e, n_xin[j], b, 1)
                        e.bn_stats(stats[:, r, :], x_in[j]).then_inc(n_stat.sem, 1)

                    def aggr(j=j, r=r):
                        wait(e, n_stat, b, 3 * j + 1, apart=True)
                        e.bn_aggr(mv[:, r, :], stats[:, r, :]).then_inc(n_stat.sem, 1)

                    def eps(j=j, r=r):
                        wait(e, n_stat, b, 3 * j + 2)
                        if j >= 2:
                            wait(e, n_norm, b, j - 1)
                        else:
                            wait(e, n_norm, b, 0)
                        e.tensor_scalar(mv[:, r, 1:2], mv[:, r, 1:2], EPS, None, ALU.add).then_inc(n_stat.sem, 1)

                    def shift(j=j, r=r):
                        wait(e, n_rstd, b, j + 1)
                        e.tensor_scalar(rs[:, r, 1:2], mv[:, r, 0:1], rs[:, r, 0:1], -1.0, ALU.mult,
                                        ALU.mult).then_inc(n_shift.sem, 1)
                    for k, f in enumerate((bn, aggr, eps)):
                        q.put(NORM[j] + AT["stats"][k], f)
                    q.put(NORM[j] + AT["shift"], shift)

            def front(q, b):
                for i in range(DT):
                    for k in range(1, TAPS):
                        def tap(i=i, k=k):
                            w = cw[:, i * TAPS + TAPS - 1 - k:i * TAPS + TAPS - k]
                            v = dtu[:, turn(b), i, k:TOK]
                            wait(e, n_tap0, b, i + 1)
                            wait(e, n_tap, b, (TAPS - 1) * i + k - 1)
                            e.scalar_tensor_tensor(out=v, in0=x_bank(b, i)[:, 0:TOK - k], scalar=w, in1=v, op0=ALU.mult,
                                                   op1=ALU.add).then_inc(n_tap.sem, 1)
                        q.put(X_TILE[i] + AT["tap"][k], tap)

                def take_c():
                    wait(e, n_cturn, b, 1)
                    wait(e, n_cnow, b, 0)
                    e.tensor_copy(c_next[:, :, :], pf[:, 0:TT * NX].rearrange("p (j x) -> p j x", j=TT)
                                  [:, :, RANK + NS:NX]).then_inc(n_cnext.sem, 1)
                q.put(X_PROJ + AT["take_c"], take_c)
                for i in range(DT):
                    def times_delta(i=i):
                        wait(e, n_delta, b, i + 1)
                        if i == 0:
                            wait(e, n_uspill, b, DT)
                            wait(e, n_xproj, b, 1)
                        e.tensor_tensor(dtu[:, turn(b), i, :], dtu[:, turn(b), i, :], delta[:, turn(b), i, :],
                                        ALU.mult).then_inc(n_dtu.sem, 1)
                    q.put(DT_TILE[i] + AT["dtu"], times_delta)

            def take_over(b):
                def task():
                    wait(e, n_cnext, b, 1)
                    wait(e, n_mac, b, 0)
                    e.tensor_copy(c_now[:, :, :], c_next[:, :, :]).then_inc(n_cnow.sem, 1)
                return task

            def back(q, b):
                for i in range(DT):
                    def silu_z(i=i):
                        wait(e, n_ztanh, b, i + 1)
                        wait(e, n_g, b, i)
                        if i == 0:
                            wait(e, n_store[0], b, 0)
                        e.scalar_tensor_tensor(out=sz[:, :], in0=sp[0][:, :], scalar=1.0, in1=pb[:, :], op0=ALU.add,
                                               op1=ALU.mult).then_inc(n_sz.sem, 1)
                    if not final(b):
                        q.put(Z_TILE[i] + AT["z_silu"], silu_z)

                    def skip(i=i):
                        wait(e, n_yturn, b, i + 1)
                        wait(e, n_side[i % 2], b, i // 2 + 1)
                        wait(e, n_g, b, i)
                        if i == 0:
                            wait(e, n_store[1], b, 0)
                        e.scalar_tensor_tensor(out=yb[:, :], in0=side[i % 2][:, :], scalar=ch[:, 2, i:i + 1],
                                               in1=y_bank(b, i)[:, :], op0=ALU.mult, op1=ALU.add).then_inc(n_y.sem, 1)
                    if final(b):
                        q.put(Z_TILE[i] + AT["skip"], skip)

                    def gate_y(i=i):
                        wait(e, n_y, b, i + 1)
                        wait(e, n_asilu, 0, i + 1)
                        e.tensor_tensor(acc_f[:, i, :, :].rearrange("p a b -> p (a b)"), yb[:, :], z_of(b, i),
                                        ALU.mult).then_inc(n_g.sem, 1)
                    if final(b):
                        q.put(Z_TILE[i] + AT["skip"], gate_y)
                for j in range(TT):
                    def silu_f(j=j):
                        wait(e, n_ftanh, b, j + 1)
                        e.scalar_tensor_tensor(out=gf[:, j, :], in0=gf[:, j, :], scalar=1.0,
                                               in1=px[:, :], op0=ALU.add, op1=ALU.mult).then_inc(n_gf.sem, 1)
                    if not final(b):
                        q.put(FFN[j] + AT["f_silu"], silu_f)

                    def gate(j=j):
                        wait(e, n_out, b, j + 1)
                        if j >= 2:
                            wait(e, n_store[j % 2], b, j // 2)
                        else:
                            wait(e, n_g, b, DT)
                        if final(b):
                            wait(e, n_asilu, 0, AHEAD)
                        else:
                            wait(e, n_gf, b, j + 1)
                        e.tensor_tensor(ob[j % 2][:, :], back_bank[j % 2][:, :], f_of(b, j), ALU.mult).then_inc(n_o.sem, 1)
                    q.put(OUT[j] + AT["out_gate"], gate)

            def ahead(q):
                for i in range(AHEAD):
                    def silu(i=i):
                        wait(e, n_atanh, 0, i + 1)
                        e.scalar_tensor_tensor(out=ahead_to(i), in0=sp[1][:, :], scalar=1.0, in1=pf[:, :], op0=ALU.add,
                                               op1=ALU.mult).then_inc(n_asilu.sem, 1)
                    q.put(AHEAD_AT[i] + AT["z_silu"] + (i >= DT) / 2, silu)

            e.memset(ones, 1.0)
            e.memset(power[:, :], -0.5).then_inc(p_dve.sem, 1)
            q = Slots()
            norm(q, 0)
            for s in range(LAST):
                q.run(s, [])
            q = Slots()
            front(q, 0)
            norm(q, 1)
            for r in range(1, FACTORS):
                def add_factor(r=r):
                    wait(e, p_f[0], 0, 1)
                    wait(e, p_f[r], 0, 1)
                    wait(e, p_fadd, 0, r - 1)
                    e.tensor_tensor(f_sb[:, :, :], f_sb[:, :, :], f_part[r], ALU.add).then_inc(p_fadd.sem, 1)
                q.put(2 * r + 6, add_factor)
            flat = [t[:, :, :, :].rearrange("p d a b -> p d (a b)") for t in (acc_f, acc)]
            stage_from, stage_to = (flat[0], flat[1], flat[0]), (flat[1], flat[0], wc_sb)
            for k in range(3):
                for i in range(DT):
                    def butterfly(k=k, i=i, d=1 << k):
                        if k == 0:
                            wait(e, p_hcopy, 0, DT)
                            wait(e, p_h, 0, DT)
                        else:
                            wait(e, p_fold, 0, DT * k)
                        lo, hi = i & ~d, i | d
                        e.tensor_tensor(stage_to[k][:, i, :], stage_from[k][:, lo, :], stage_from[k][:, hi, :],
                                        ALU.subtract if i & d else ALU.add).then_inc(p_fold.sem, 1)
                    q.put(1 + 2 * k + i / 8 if k else 1.75, butterfly)
            for s in range(LAST):
                q.run(s, [])
            def round_(t, has_front, has_norm, has_back):
                q = fill(t, has_front, has_norm, has_back, front, norm, back, ahead)
                for s in range(STEPS):
                    if s == 0:
                        macs = [mac(t - 1, STEPS - 1, j) for j in range(TT)] if has_back else []
                    else:
                        macs = [mac(t, s - 1, j) for j in range(TT)]
                    own = [scan(t, s, i) for i in range(HALF)]
                    own = [task for pair in zip(own, macs) for task in pair] if macs else own
                    if s == 1:
                        own = [take_over(t)] + own
                    q.run(s, own)

            rounds(e, round_)
            for j in range(TT):
                mac(BATCH - 1, STEPS - 1, j)()
            q = fill(BATCH, False, False, True, None, None, back, None)
            for s in range(LAST):
                q.run(s, [])

        @block.sync
        def _(e):
            def b_load(b, n):
                def task():
                    if n == 0:
                        wait(e, n_bspill, b, 1)
                    wait(e, n_dbu, b, 4 * (n - 1))
                    src = b_dram[b, n:n + 1, :].broadcast_to([P, TOK])
                    e.dma_start(b_rep[n % 2][:, :], src).then_inc(n_brep[n % 2].sem, 16)
                return task

            def norm(q, b):
                for j in range(TT):
                    def load(j=j):
                        if j < 2:
                            wait(e, n_in, b, 0)
                        elif not isinstance(b, int) or b > 2:
                            wait(e, n_z, b - 2, 0)
                        e.dma_start(x_in[j], x[b, j * P:(j + 1) * P, :]).then_inc(n_xin[j].sem, 16)
                    q.put(NORM[j] - 3, load)

                for i in range(2):
                    def load_w(i=i):
                        wait(e, n_xturn, b, i + 1)
                        e.dma_start(w_xt[i][:, :, :].rearrange("p a b -> p (a b)"), w_in[i]).then_inc(n_wx[i].sem, 16)
                    q.put(NORM[i] + 1.25, load_w)

                def spill():
                    wait(e, n_xnt, b, TT)
                    e.dma_start(xn_dram[b], xnt[:, :, :].rearrange("p a b -> p (a b)")).then_inc(n_xspill.sem, 16)
                q.put(NORM[-1] + 1.99, spill)

            def front(q, b):
                for i in range(DT):
                    def load(i=i):
                        wait(e, n_in, b, i - 1)
                        e.dma_start(w_xt[i % 2][:, :, :].rearrange("p a b -> p (a b)"),
                                    w_in[i]).then_inc(n_wx[i % 2].sem, 16)
                    if i >= 2:
                        q.put(X_TILE[i] - 1.5, load)

                    def spill(i=i):
                        wait(e, n_u, b, i + 1)
                        e.dma_start(u_dram[b, i], dtu[:, turn(b), i, :]).then_inc(n_uspill.sem, 16)
                    q.put(X_TILE[i] + AT["x_silu"] - .5, spill)

                def spill_b():
                    wait(e, n_xdbl, b, 1)
                    e.dma_start(b_dram[b], xdbl[RANK:RANK + NS, :]).then_inc(n_bspill.sem, 16)
                q.put(X_PROJ + AT["take_xdbl"] - .5, spill_b)

            def back(q, b):
                def load_xn():
                    wait(e, n_xspill, b, 1)
                    wait(e, n_ffn, b, 0)
                    e.dma_start(xnt_b[:, :, :].rearrange("p a b -> p (a b)"), xn_dram[b]).then_inc(n_xback.sem, 16)
                if not final(b):
                    q.put(0, load_xn)
                for i in range(DT):
                    def load(i=i):
                        if i < 2:
                            wait(e, n_xturn, b + 3 if not isinstance(b, int) else min(b + 3, BATCH), 0)
                        else:
                            wait(e, n_z, b, i - 1)
                        e.dma_start(w_zt[i % 2][:, :, :].rearrange("p a b -> p (a b)"),
                                    w_in[DT + i]).then_inc(n_wz[i % 2].sem, 16)
                    if not final(b):
                        q.put(max(0, Z_TILE[i] - 1.5), load)

                    def side_u(i=i):
                        if i == 0:
                            wait(e, n_uspill, b, DT)
                            wait(e, n_sum, b, 0)
                        if i >= 2:
                            wait(e, n_g, b, i - 1)
                        e.dma_start(side[i % 2][:, :], u_dram[b, i]).then_inc(n_side[i % 2].sem, 16)
                    q.put(Z_TILE[i] + .25, side_u)
                for j in range(TT):
                    def side_x(j=j):
                        if j < 2:
                            wait(e, n_g, b, DT)
                        else:
                            wait(e, n_sum, b, j - 1)
                        e.dma_start(side[j % 2][:, :], x[b, j * P:(j + 1) * P, :]).then_inc(n_side[j % 2].sem, 16)
                    q.put(OUT[j] + 1, side_x)

                    def store(j=j):
                        wait(e, n_sum, b, j + 1)
                        e.dma_start(out[b, j * P:(j + 1) * P, :], ob[j % 2][:, :]).then_inc(n_store[j % 2].sem, 16)
                    q.put(OUT[j] + AT["residual"] - .5, store)

            def ahead(q):
                for i in range(DT):
                    def load(i=i):
                        if i < 2:
                            wait(e, n_in, BATCH, 0)
                        else:
                            wait(e, n_a, 0, i - 1)
                        e.dma_start(w_xt[i % 2][:, :, :].rearrange("p a b -> p (a b)"),
                                    w_in[DT + i]).then_inc(n_aload[i % 2].sem, 16)
                    q.put(max(0, AHEAD_AT[i] - 1.5), load)

            loads = [(ident[:, :], consts[0]), (ident_had, consts[1]),
                     (wx_sb[:, :, :].rearrange("p a b -> p (a b)"), w_x), (wdt_sb[0:RANK, :], w_dt), (a_sb[:, :], a_log),
                     (cw[:, :], conv_w), (ch[:, :, :].rearrange("p a b -> p (a b)"), chan), (bias_sb, bias)]
            assert len(loads) == LOADS
            for to, src in loads:
                e.dma_start(to, src).then_inc(p_load.sem, 16)
            q = Slots()
            norm(q, 0)
            spill = q.at.pop(int(NORM[-1] + 1.99))
            for s in range(LAST):
                q.run(s, [])
            for i in range(2):
                e.dma_start(acc[:, i * HALF:(i + 1) * HALF, :, :].rearrange("p d a b -> p (d a b)"),
                            w_out[:, i * HALF * DM:(i + 1) * HALF * DM]).then_inc(p_wout.sem, 16)
            for _, task in spill:
                task()
            q = Slots()
            front(q, 0)
            norm(q, 1)
            for r in range(FACTORS):
                def load_factor(r=r):
                    e.dma_start(f_part[r], factors[r].rearrange("p (a b) -> p a b", a=KT)).then_inc(p_f[r].sem, 16)
                q.put(2 + 2 * r, load_factor)
            q.put(X_PROJ + AT["take_xdbl"], b_load(0, 0))
            for s in range(LAST):
                q.run(s, [])

            def round_(t, has_front, has_norm, has_back):
                q = fill(t, has_front, has_norm, has_back, front, norm, back, ahead)
                for n in range(1, NS):
                    q.put(max(0, 2 * n - 2.5), b_load(t, n))
                if has_front:
                    q.put(STEPS - .1, b_load(t + 1, 0))
                for s in range(STEPS):
                    q.run(s, [])

            rounds(e, round_)
            q = fill(BATCH, False, False, True, None, None, back, None)
            for s in range(LAST):
                q.run(s, [])
            for i in range(2):
                wait(e, n_store[i], BATCH - 1, TT // 2)


def kernel(**inputs):
    from concourse import bacc
    from concourse.bass_utils import run_bass_kernel_spmd

    a = {k.removeprefix("L0_attn_"): np.asarray(v) for k, v in inputs.items()}

    def tiles(v, n):
        return np.ascontiguousarray(v.reshape(n, P, -1).transpose(1, 0, 2).reshape(P, -1))

    h = np.array([[1.0]])
    while h.shape[0] < P:
        h = np.block([[h, h], [h, -h]])
    had = (h / (4 * DI ** 0.5)).astype(np.float32)
    w_in = a["W_in"]
    arrays = {
        "x": a["hidden_states"],
        "w_in": np.ascontiguousarray(w_in.reshape(2 * DT, P, KT, P).transpose(0, 3, 2, 1).reshape(2 * DT, P, KT * P)),
        "w_x": tiles(a["W_x"].T, DT),
        "w_dt": np.ascontiguousarray(a["W_dt"].T),
        "w_out": tiles(a["W_out"].T, DT),
        "a_log": tiles(a["A_log"], DT),
        "conv_w": tiles(a["conv_w"], DT),
        "chan": np.concatenate([tiles(a[n].reshape(-1, 1), DT) for n in ("conv_b", "dt_bias", "D")], axis=1),
        "factors": np.ascontiguousarray(a["L0_ffn_factors"].reshape(FACTORS, KT, P, DM).transpose(0, 2, 1, 3)
                                        .reshape(FACTORS, P, KT * DM)),
        "bias": a["L0_ffn_bias"].reshape(1, DM),
        "consts": np.stack([np.eye(P, dtype=np.float32), had]),
    }
    nc = bacc.Bacc("TRN2", target_bir_lowering=False, num_devices=1)
    ap = {n: nc.dram_tensor(f"in_{n}", v.shape, F32, kind="ExternalInput").ap() for n, v in arrays.items()}
    u_dram = nc.dram_tensor("u_dram", [BATCH, DT, P, TOK], F32, kind="Internal").ap()
    xn_dram = nc.dram_tensor("xn_dram", [BATCH, P, KT * TOK], F32, kind="Internal").ap()
    b_dram = nc.dram_tensor("b_dram", [BATCH, NS, TOK], F32, kind="Internal").ap()
    out = nc.dram_tensor("out", [BATCH, TOK, DM], F32, kind="ExternalOutput").ap()
    program(nc, ap["x"], ap["w_in"], ap["w_x"], ap["w_dt"], ap["w_out"], ap["a_log"], ap["conv_w"], ap["chan"],
            ap["factors"], ap["bias"], ap["consts"], u_dram, xn_dram, b_dram, out)
    r = run_bass_kernel_spmd(nc, [{f"in_{n}": v for n, v in arrays.items()}], core_ids=[0])
    return r.results[0]["out"]
```
